# Optimizing a Trainium2 kernel written in Bass

```python
import numpy as np
import jax
import jax.numpy as jnp

def _softmax(x, axis=-1):
    return jax.nn.softmax(x, axis=axis)

def _gelu(x):
    return jax.nn.gelu(x, approximate=True)

def _silu(x):
    return jax.nn.silu(x)

def _sigmoid(x):
    return jax.nn.sigmoid(x)

def _layernorm(x, axis=-1, eps=1e-05):
    m = jnp.mean(x, axis=axis, keepdims=True)
    v = jnp.var(x, axis=axis, keepdims=True)
    return (x - m) / jnp.sqrt(v + eps)

def _scatter_add(tgt, idx, src, axis=0):
    return tgt.at[idx].add(src)

def _segment_sum(src, seg, n):
    return jax.ops.segment_sum(src, seg, n)
kernel_name = 'mk_gps_d1_gnn_r8_be47ee'

def setup_inputs(seed: int=0):
    np.random.seed(seed)
    _w = jnp.asarray

    def _rec_inputs():
        import jax
        import jax.numpy as jnp
        _gk = jax.random.key(seed)
        x = -0.0003713 + 1 * jax.random.normal(jax.random.fold_in(_gk, 1), (6250, 256), jnp.float32)
        _s = jax.random.randint(jax.random.fold_in(_gk, 2), (50000,), 0, 6250, jnp.int32)
        _d = jax.random.randint(jax.random.fold_in(_gk, 3), (50000,), 0, 6250, jnp.int32)
        _loop = jnp.arange(6250, dtype=jnp.int32)
        src = jnp.concatenate([_s, _d, _loop])
        dst = jnp.concatenate([_d, _s, _loop])
        _o = jnp.argsort(dst, stable=True)
        src = src[_o]
        dst = dst[_o]
        return (x, src, dst)
    x, src, dst = _rec_inputs()

    def _L0_gnn_setup():
        import jax, jax.numpy as jnp
        import numpy as np
        N, IN_CH, HEADS, OUT_CH, E = (6250, 256, 4, 64, 100000)
        key = jax.random.key(seed)
        k1, k2, k3, k4, k5 = jax.random.split(key, 5)
        x = jax.random.normal(k1, (N, IN_CH), dtype=jnp.float32)
        edge_index = jax.random.randint(k2, (2, E), 0, N, dtype=jnp.int64)
        bw = float(np.sqrt(6.0 / (IN_CH + HEADS * OUT_CH)))
        ba = float(np.sqrt(6.0 / (HEADS + OUT_CH)))
        weight = jax.random.uniform(k3, (IN_CH, HEADS * OUT_CH), jnp.float32, -bw, bw)
        attn_l = jax.random.uniform(k4, (HEADS, OUT_CH), jnp.float32, -ba, ba)
        attn_r = jax.random.uniform(k5, (HEADS, OUT_CH), jnp.float32, -ba, ba)
        return {'x': x, 'edge_index': edge_index, 'weight': weight, 'attn_l': attn_l, 'attn_r': attn_r}
    _L0_gnn_all = _L0_gnn_setup()
    _L0_gnn_in = {k: v for k, v in _L0_gnn_all.items() if k in ('weight', 'attn_l', 'attn_r')}
    del _L0_gnn_all

    def _L0_mix_setup():
        import jax, jax.numpy as jnp
        import numpy as np
        MIDC = 256
        HEADS = 8
        HEADC = MIDC // HEADS
        EPS = 1e-05

        def _ln(x, gamma, beta):
            mu = jnp.mean(x, axis=-1, keepdims=True)
            var = jnp.var(x, axis=-1, keepdims=True)
            return (x - mu) * jax.lax.rsqrt(var + EPS) * gamma + beta
        key = jax.random.key(seed)
        ks = jax.random.split(key, 8)
        B, HW, C = (8, 512, MIDC)
        s = 1.0 / np.sqrt(C)
        return {'x': jax.random.normal(ks[0], (B, HW, C), jnp.float32), 'w_qkv': jax.random.normal(ks[1], (C, 3 * C), jnp.float32) * s, 'b_qkv': jnp.zeros((3 * C,), jnp.float32), 'kln_g': jnp.ones((HEADC,), jnp.float32), 'kln_b': jnp.zeros((HEADC,), jnp.float32), 'vln_g': jnp.ones((HEADC,), jnp.float32), 'vln_b': jnp.zeros((HEADC,), jnp.float32), 'w1': jax.random.normal(ks[2], (C, C), jnp.float32) * s, 'b1': jnp.zeros((C,), jnp.float32), 'w2': jax.random.normal(ks[3], (C, C), jnp.float32) * s, 'b2': jnp.zeros((C,), jnp.float32)}
    _L0_mix_all = _L0_mix_setup()
    _L0_mix_in = {k: v for k, v in _L0_mix_all.items() if k in ('w_qkv', 'b_qkv', 'kln_g', 'kln_b', 'vln_g', 'vln_b', 'w1', 'b1', 'w2', 'b2')}
    del _L0_mix_all

    def _L0_ffn_setup():
        import jax, jax.numpy as jnp
        import numpy as np
        BN_EPS = 0.001

        def _bn(h, g, b, m, v):
            return g * (h - m) * jax.lax.rsqrt(v + BN_EPS) + b
        key = jax.random.key(seed)
        ks = jax.random.split(key, 8)
        B, F, Df = (256, 64, 256)
        E, H, D = (8, 256, 256)
        s1 = 1.0 / np.sqrt(Df)
        s2 = 1.0 / np.sqrt(H)
        return {'x': jax.random.normal(ks[0], (B, F, Df), jnp.float32), 'Wr': jax.random.normal(ks[1], (Df, E), jnp.float32) * s1, 'br': jnp.zeros((E,), jnp.float32), 'W1': jax.random.normal(ks[2], (E, Df, H), jnp.float32) * s1, 'b1': jnp.zeros((E, H), jnp.float32), 'g1': jnp.ones((E, H), jnp.float32), 'be1': jnp.zeros((E, H), jnp.float32), 'm1': jnp.zeros((E, H), jnp.float32), 'v1': jnp.ones((E, H), jnp.float32), 'W2': jax.random.normal(ks[3], (E, H, H), jnp.float32) * s2, 'b2': jnp.zeros((E, H), jnp.float32), 'g2': jnp.ones((E, H), jnp.float32), 'be2': jnp.zeros((E, H), jnp.float32), 'm2': jnp.zeros((E, H), jnp.float32), 'v2': jnp.ones((E, H), jnp.float32), 'Wo': jax.random.normal(ks[4], (E, H, D), jnp.float32) * s2, 'bo': jnp.zeros((E, D), jnp.float32)}
    _L0_ffn_all = _L0_ffn_setup()
    _L0_ffn_in = {k: v for k, v in _L0_ffn_all.items() if k in ('Wr', 'br', 'W1', 'b1', 'g1', 'be1', 'm1', 'v1', 'W2', 'b2', 'g2', 'be2', 'm2', 'v2', 'Wo', 'bo')}
    del _L0_ffn_all
    return {'x': x, 'src': src, 'dst': dst, 'L0_gnn_weight': _L0_gnn_in['weight'], 'L0_gnn_attn_l': _L0_gnn_in['attn_l'], 'L0_gnn_attn_r': _L0_gnn_in['attn_r'], 'L0_mix_w_qkv': _L0_mix_in['w_qkv'], 'L0_mix_b_qkv': _L0_mix_in['b_qkv'], 'L0_mix_kln_g': _L0_mix_in['kln_g'], 'L0_mix_kln_b': _L0_mix_in['kln_b'], 'L0_mix_vln_g': _L0_mix_in['vln_g'], 'L0_mix_vln_b': _L0_mix_in['vln_b'], 'L0_mix_w1': _L0_mix_in['w1'], 'L0_mix_b1': _L0_mix_in['b1'], 'L0_mix_w2': _L0_mix_in['w2'], 'L0_mix_b2': _L0_mix_in['b2'], 'L0_ffn_Wr': _L0_ffn_in['Wr'], 'L0_ffn_br': _L0_ffn_in['br'], 'L0_ffn_W1': _L0_ffn_in['W1'], 'L0_ffn_b1': _L0_ffn_in['b1'], 'L0_ffn_g1': _L0_ffn_in['g1'], 'L0_ffn_be1': _L0_ffn_in['be1'], 'L0_ffn_m1': _L0_ffn_in['m1'], 'L0_ffn_v1': _L0_ffn_in['v1'], 'L0_ffn_W2': _L0_ffn_in['W2'], 'L0_ffn_b2': _L0_ffn_in['b2'], 'L0_ffn_g2': _L0_ffn_in['g2'], 'L0_ffn_be2': _L0_ffn_in['be2'], 'L0_ffn_m2': _L0_ffn_in['m2'], 'L0_ffn_v2': _L0_ffn_in['v2'], 'L0_ffn_Wo': _L0_ffn_in['Wo'], 'L0_ffn_bo': _L0_ffn_in['bo']}

def reference(x, src, dst, L0_gnn_weight, L0_gnn_attn_l, L0_gnn_attn_r, L0_mix_w_qkv, L0_mix_b_qkv, L0_mix_kln_g, L0_mix_kln_b, L0_mix_vln_g, L0_mix_vln_b, L0_mix_w1, L0_mix_b1, L0_mix_w2, L0_mix_b2, L0_ffn_Wr, L0_ffn_br, L0_ffn_W1, L0_ffn_b1, L0_ffn_g1, L0_ffn_be1, L0_ffn_m1, L0_ffn_v1, L0_ffn_W2, L0_ffn_b2, L0_ffn_g2, L0_ffn_be2, L0_ffn_m2, L0_ffn_v2, L0_ffn_Wo, L0_ffn_bo):
    import jax
    import jax.numpy as jnp

    def _L0_gnn_ref(x, edge_index, weight, attn_l, attn_r):
        import jax, jax.numpy as jnp
        import numpy as np
        N, IN_CH, HEADS, OUT_CH, E = (6250, 256, 4, 64, 100000)
        heads, out_ch = attn_l.shape
        n = x.shape[0]
        xt = jnp.matmul(x, weight).reshape(-1, heads, out_ch)
        row, col = (edge_index[0], edge_index[1])
        alpha_l = jnp.einsum('ehd,hd->eh', xt[row], attn_l)
        alpha_r = jnp.einsum('ehd,hd->eh', xt[col], attn_r)
        alpha = jax.nn.softmax(jax.nn.leaky_relu(alpha_l + alpha_r, 0.01), axis=1)
        tmp = jnp.einsum('nh,nhd->nd', alpha[:n], xt[col[:n]])
        out = jnp.broadcast_to(tmp[:, None, :], (n, heads, out_ch))
        return out.reshape(n, heads * out_ch)

    def _L0_mix_ref(x, w_qkv, b_qkv, kln_g, kln_b, vln_g, vln_b, w1, b1, w2, b2):
        import jax, jax.numpy as jnp
        import numpy as np
        MIDC = 256
        HEADS = 8
        HEADC = MIDC // HEADS
        EPS = 1e-05

        def _ln(x, gamma, beta):
            mu = jnp.mean(x, axis=-1, keepdims=True)
            var = jnp.var(x, axis=-1, keepdims=True)
            return (x - mu) * jax.lax.rsqrt(var + EPS) * gamma + beta
        B, HW, C = x.shape
        bias = x
        qkv = (x @ w_qkv + b_qkv).reshape(B, HW, HEADS, 3 * HEADC)
        qkv = qkv.transpose(0, 2, 1, 3)
        q, k, v = jnp.split(qkv, 3, axis=-1)
        k = _ln(k, kln_g, kln_b)
        v = _ln(v, vln_g, vln_b)
        kv = jnp.einsum('bhnd,bhne->bhde', k, v) / HW
        out = jnp.einsum('bhnd,bhde->bhne', q, kv)
        out = out.transpose(0, 2, 1, 3).reshape(B, HW, C)
        ret = out + bias
        h = jax.nn.gelu(ret @ w1 + b1, approximate=False)
        return h @ w2 + b2 + bias

    def _L0_ffn_ref(x, Wr, br, W1, b1, g1, be1, m1, v1, W2, b2, g2, be2, m2, v2, Wo, bo):
        import jax, jax.numpy as jnp
        import numpy as np
        BN_EPS = 0.001

        def _bn(h, g, b, m, v):
            return g * (h - m) * jax.lax.rsqrt(v + BN_EPS) + b
        feat = jnp.mean(x, axis=0)
        w = jax.nn.softmax(feat @ Wr + br, axis=-1)
        h = jnp.einsum('bfd,edh->bfeh', x, W1) + b1
        h = jax.nn.relu(_bn(h, g1, be1, m1, v1))
        h = jnp.einsum('bfeh,ehk->bfek', h, W2) + b2
        h = jax.nn.relu(_bn(h, g2, be2, m2, v2))
        y = jnp.einsum('bfeh,ehd->bfed', h, Wo) + bo
        return jnp.einsum('bfed,fe->bfd', y, w)
    edge_index = jnp.stack([src, dst])
    xn = _layernorm(x, axis=-1)
    x = x + _L0_gnn_ref(xn, edge_index, L0_gnn_weight, L0_gnn_attn_l, L0_gnn_attn_r) + _L0_mix_ref(xn[None], L0_mix_w_qkv, L0_mix_b_qkv, L0_mix_kln_g, L0_mix_kln_b, L0_mix_vln_g, L0_mix_vln_b, L0_mix_w1, L0_mix_b1, L0_mix_w2, L0_mix_b2)[0]
    x = x + _L0_ffn_ref(_layernorm(x, axis=-1)[None], L0_ffn_Wr, L0_ffn_br, L0_ffn_W1, L0_ffn_b1, L0_ffn_g1, L0_ffn_be1, L0_ffn_m1, L0_ffn_v1, L0_ffn_W2, L0_ffn_b2, L0_ffn_g2, L0_ffn_be2, L0_ffn_m2, L0_ffn_v2, L0_ffn_Wo, L0_ffn_bo)[0]
    return x

_drawn_inputs = setup_inputs


def setup_inputs(seed=0):
    import zlib

    import numpy as np

    out = dict(_drawn_inputs(seed))
    spreads = {'L0_mix_b_qkv': (0.0, 0.273),
     'L0_mix_kln_g': (1.0, 0.6),
     'L0_mix_kln_b': (0.0, 0.462),
     'L0_mix_vln_g': (1.0, 0.6),
     'L0_mix_vln_b': (0.0, 0.414),
     'L0_mix_b1': (0.0, 0.269),
     'L0_mix_b2': (0.0, 0.1),
     'L0_ffn_br': (0.0, 0.501),
     'L0_ffn_b1': (0.0, 0.699),
     'L0_ffn_g1': (1.0, 0.6),
     'L0_ffn_be1': (0.0, 0.706),
     'L0_ffn_m1': (0.0, 0.691),
     'L0_ffn_v1': (1.0, 0.6),
     'L0_ffn_b2': (0.0, 0.494),
     'L0_ffn_g2': (1.0, 0.6),
     'L0_ffn_be2': (0.0, 0.522),
     'L0_ffn_m2': (0.0, 0.516),
     'L0_ffn_v2': (1.0, 0.6),
     'L0_ffn_bo': (0.0, 0.373)}
    factors = {}
    for name, (base, spread) in spreads.items():
        noise = np.random.default_rng([zlib.crc32(name.encode()), seed]).standard_normal(out[name].shape)
        drawn = base * np.exp(spread * noise) if base else spread * noise
        out[name] = jnp.asarray(drawn.astype(out[name].dtype))
    for name, factor in factors.items():
        out[name] = (out[name] * factor).astype(out[name].dtype)
    return out
```

```python
import concourse.bass as bass
from concourse import mybir
from contextlib import ExitStack

fp32 = mybir.dt.float32
f32r = mybir.dt.float32r
i32 = mybir.dt.int32
ALU = mybir.AluOpType
ACT = mybir.ActivationFunctionType
AX = mybir.AxisListType

N, D = 6250, 256
P = 128
KT = D // P
CH = 512
TPC = CH // P
NFULL = N // CH
TAIL = N - NFULL * CH
NH, HC = 8, 32
GH, GC = 4, 64
NE = 8
NG = 2 * NH
TAB = D + GH
XTW = D + 2 * GH
WA = 2 * D + XTW
LN_EPS, BN_EPS = 1e-5, 1e-3


class Chunk:

    def __init__(self, c, half, par, rows=CH):
        self.c, self.half, self.par, self.rows = c, half, par, rows
        self.nt = (rows + P - 1) // P
        self.tp = min(rows, P)
        self.last = rows != CH

    @staticmethod
    def at(c):
        return Chunk(c, c // 2, c % 2, CH if c < NFULL else TAIL)

    def next(self):
        if isinstance(self.c, int):
            return Chunk.at(self.c + 1)
        return Chunk(self.c + 1, self.half + self.par, 1 - self.par)

    def prev(self):
        if isinstance(self.c, int):
            return Chunk.at(self.c - 1)
        return Chunk(self.c - 1, self.half - (1 - self.par), 1 - self.par)

    def rows_of(self, dram, nt=None):
        part = dram[bass.ds(self.c * CH, self.rows), :]
        return part.rearrange("(t p) d -> p t d", p=self.tp)


def need(eng, sem, value, alone=None):
    if isinstance(value, int):
        if value > 0:
            eng.wait_ge(sem, value)
        return
    eng.wait_ge(sem, value)
    if alone is not None:
        eng.sem_inc(alone, 1)


class Chain:

    def __init__(self, eng, sem, base=0, alone=None):
        self.eng, self.sem, self.base, self.n, self.alone = eng, sem, base, 0, alone

    def step(self, ins):
        ins.then_inc(self.sem, 1)
        self.n += 1
        need(self.eng, self.sem, self.base + self.n, self.alone)


def build(nc, I, out):
    ctx = ExitStack()
    with ctx:
        def sb(name, shape, dt=fp32):
            return ctx.enter_context(nc.sbuf_tensor(name, shape, dt))

        def sem(name):
            return ctx.enter_context(nc.semaphore(name))

        tab_d = nc.dram_tensor("node_table", (N, TAB), fp32).ap()
        al_d = nc.dram_tensor("node_alpha_l", (N, GH), fp32).ap()

        whi = sb("ffn_w_high", [P, 3 * NE, KT * D], f32r)
        wlo = sb("ffn_w_low", [P, 3 * NE, KT * D], f32r)
        h1h = sb("h1_high", [P, 2, 2, CH], f32r)
        h1l = sb("h1_low", [P, 2, 2, CH], f32r)
        h2h = sb("h2_high", [P, 2, CH], f32r)
        h2l = sb("h2_low", [P, 2, CH], f32r)
        tmp = sb("activated", [P, 3, CH])
        xTh = sb("xT_high", [P, 2, KT, CH], f32r)
        xTl = sb("xT_low", [P, 2, KT, CH], f32r)
        xmh = sb("mix_xT_high", [P, KT, CH], f32r)
        xml = sb("mix_xT_low", [P, KT, CH], f32r)
        hmh, hml = xmh, xml
        mwh = sb("mix_w_high", [P, 2, KT, D], f32r)
        mwl = sb("mix_w_low", [P, 2, KT, D], f32r)
        xb = sb("x_rows", [P, 2, TPC, D])
        acc = sb("accumulated", [P, 2, TPC, D])
        xn = sb("normalised", [P, TPC, D])
        base = sb("residual", [P, TPC, D])
        G = sb("gathered", [P, TPC * TAB])
        wst = sb("weight_stage", [P, 3, KT * D])
        wAh = h1h[:, :, :, :].rearrange("p a b c -> p (a b c)")[:, 0:KT * WA].rearrange("p (k n) -> p k n", k=KT)
        wAl = h1l[:, :, :, :].rearrange("p a b c -> p (a b c)")[:, 0:KT * WA].rearrange("p (k n) -> p k n", k=KT)
        kvh, kvl = h2h, h2l
        kvn, sq = tmp[:, 0:2, :], tmp[:, 2, :]
        accf = acc[:, :, :, :].rearrange("p a b c -> p (a b c)")
        wqkv = accf[:, 0:KT * 3 * D].rearrange("p (k n) -> p k n", k=KT)
        w1m = accf[:, KT * 3 * D:KT * 4 * D].rearrange("p (k n) -> p k n", k=KT)
        basef = base[:, :, :].rearrange("p a b -> p (a b)")
        wqT = basef[:, 0:KT * D].rearrange("p (k n) -> p k n", k=KT)
        Pm = basef[:, KT * D:2 * KT * D].rearrange("p (k n) -> p k n", k=KT)
        kvT = xn[:, 2, :].rearrange("p (g n) -> p g n", g=2)
        kvsum = G[:, 0:2 * D]
        xte = G[:, 2 * D:2 * D + 2 * XTW].rearrange("p (a n) -> p a n", a=2)
        Gt = G[:, :].rearrange("p (t n) -> p t n", t=TPC)

        ident = sb("identity", [P, P])
        onesf = sb("ones", [P, P])
        onesr = sb("ones_r", [P, P], f32r)
        brow = sb("kv_bias_rows", [P, 2 * D], f32r)
        bo3 = sb("bo_rows", [P, D], f32r)
        wrh = sb("router_w_high", [P, KT, NE], f32r)
        wrl = sb("router_w_low", [P, KT, NE], f32r)
        w3T = sb("router_wT", [P, TPC, P], f32r)
        w3 = sb("router_w3", [P, TPC, P])
        b2bc = sb("b2_rows", [P, D])
        brbc = sb("br_rows", [P, NE])
        bnp = sb("bn_cols", [P, 2, 2, 2 * NE])
        c1c = sb("mix_bias_cols", [P, 2])
        b1c = sb("b1_cols", [P, 2])
        bqc = sb("bq_cols", [P, KT])
        gkb = sb("k_gain_rows", [P, HC])
        bkb = sb("k_shift_rows", [P, HC])
        gvc = sb("v_gain_col", [P, 1])
        bvc = sb("v_shift_col", [P, 1])
        mhalf = sb("minus_half", [P, NG])
        rsA = sb("rstd_all", [P, TPC * (NFULL + 1)])
        nmA = sb("shift_all", [P, TPC * (NFULL + 1)])
        st6 = sb("bn_stats", [P, TPC, 6])
        mv = sb("mean_var", [P, TPC, 2])
        rs = sb("rstd", [P, 2, TPC])
        nm = sb("shift", [P, 2, TPC])
        epsc = sb("eps_cols", [P, 2])
        rs1 = sb("rstd_plus_one", [P, TPC])
        ss = sb("sum_squares", [P, 2, NG])
        rk = sb("kv_rstd", [P, 2, NG])
        mn = sb("group_means", [P, NG])
        idx = sb("indices", [P, 2, TPC], i32)
        gal = sb("alpha_l", [P, TPC * GH])
        ga = sb("graph_logits", [P, TPC, GH])
        gs = sb("graph_scalars", [P, 2, TPC])
        rl = sb("router_logits", [P, TPC, NE])
        rq = sb("router_scalars", [P, 2, TPC])
        wpar = [sb(f"router_w{i}", [P, TPC, NE]) for i in range(2)]
        rhr = sb("router_high", [P, TPC, NE], f32r)
        bnr = sb("bn_rows", [4 * NE, 5, P])

        bank = [ctx.enter_context(nc.psum_tensor(f"bank{i}", [P, 512], fp32)) for i in range(8)]
        KVb, XTb, Tb, Sb = bank[0:2], bank[2:4], bank[4:6], bank[6:8]
        L1b, L2b, Yb, Fb = bank[0:2], bank[2:4], bank[4:6], bank[6:8]

        names = """ld_w ld_bn ld_small ld_stage id ones eps set_dve set_act set_pool set_pe
            bn_t bn_ev wq_t wq_ev wst_ld wst_hi wst_lo
            bn_sq bn_rc x0 x1 stat xsd xrec rstd xnorm tr thi tlo kv xt sq ssum krs krec kvn kvhi kvlo ksum S xte tab0 tab1
            mid_pe mid_dve
            rsl xB0 xB1 fxn fT fThi fTlo fm1 gelu fmh fm2 fx2 fst frs fx2n f2T f2hi f2lo frt flg fex fw3 fw3T fw3c fbo fai
            idx gath glog gexp galpha gbase dsm
            l1 r1 hi1 h1 l2 r2 hi2 h2 y acc out0 out1 passed_pool passed_dve passed_sp""".split()
        s = {n: sem("s_" + n) for n in names}
        s_x = [s["x0"], s["x1"]]
        s_xB = [s["xB0"], s["xB1"]]
        s_tab = [s["tab0"], s["tab1"]]
        s_out = [s["out0"], s["out1"]]

        chunk = Chunk.at
        LAST = chunk(NFULL)
        NTILES = TPC * NFULL + 1

        def mm3(dst, lhs, rhs, lead=False):
            last = None
            n = len(lhs)
            for k in range(n):
                (ah, al), (bh, bl) = lhs[k], rhs[k]
                nc.tensor.matmul(dst, ah, bh, start=(k == 0 and not lead), stop=False)
                nc.tensor.matmul(dst, ah, bl, start=False, stop=False)
                last = nc.tensor.matmul(dst, al, bh, start=False, stop=(k == n - 1))
            return last

        def wide(ap, shape):
            return ap.unsqueeze(len(ap.shape)).broadcast_to(shape)

        def pair(j):
            return Chunk(2 * j + 1, j, 1), Chunk(2 * j + 2, j + 1, 0)

        def phase_a_loop(eng, step, ahead=1):
            step(chunk(0), 0)
            with eng.Fori(0, (NE - 2) // 2) as j:
                for ch in pair(j):
                    step(ch, ch.c)
            if ahead == 1:
                with eng.Fori((NE - 2) // 2, NFULL // 2 - 1) as j:
                    for ch in pair(j):
                        step(ch, None)
            else:
                for c in range(NE - 1, NFULL - 1):
                    step(chunk(c), None)
            step(chunk(NFULL - 1), NE - 1)
            step(LAST, None)

        def phase_b_loop(eng, step, ahead=1):
            step(chunk(0))
            rounds = NFULL // 2 - ahead
            with eng.Fori(0, rounds) as j:
                for ch in pair(j):
                    step(ch)
            for c in range(2 * rounds + 1, NFULL + 1):
                step(chunk(c))

        STAT_TURN = {0: (0, 1), 1: (2, 3)}
        TURN = {2: (0, 1), 3: (2, 3)}

        def of_next(ch, t, turns):
            if ch.last:
                return []
            return [u for u in turns.get(t, ()) if u < ch.next().nt]

        SETUP_A, SETUP_Q, SETUP_ALL = 42, 44, 50
        LD_SMALL = 27
        MID_KV, MID_P, MID = 23, 24, 30

        block = ctx.enter_context(nc.Block())

        @block.sync
        def _(sp):
            def load_x(ch, sems, seen):
                if seen is not None:
                    need(sp, *seen)
                sp.dma_start(xb[0:ch.tp, ch.par, 0:ch.nt, :], ch.rows_of(I["x"])).then_inc(sems[ch.par], 16)

            load_x(chunk(0), s_x, None)
            sp.dma_start(wqkv, I["L0_mix_w_qkv"].rearrange("(k p) n -> p k n", p=P)).then_inc(s["ld_w"], 16)
            sp.dma_start(wst[:, 0, :].rearrange("p (k n) -> p k n", k=KT),
                         I["L0_gnn_weight"].rearrange("(k p) n -> p k n", p=P)).then_inc(s["ld_w"], 16)
            sp.dma_start(wst[:, 1, 0:D], I["L0_gnn_attn_r"].rearrange("a b -> (a b)").partition_broadcast(P)).then_inc(s["ld_w"], 16)
            sp.dma_start(wst[:, 1, D:2 * D], I["L0_gnn_attn_l"].rearrange("a b -> (a b)").partition_broadcast(P)).then_inc(s["ld_w"], 16)
            sp.dma_start(tmp[0:2, 0:2, :].rearrange("p a b -> p (a b)")[:, 0:3 * D],
                         I["L0_mix_b_qkv"].partition_broadcast(2)).then_inc(s["ld_w"], 16)
            load_x(chunk(1), s_x, None)
            for i, n in enumerate(("b1", "g1", "be1", "m1", "v1")):
                for l in range(2):
                    name = "L0_ffn_" + n.replace("1", str(l + 1))
                    sp.dma_start(bnr[2 * NE * l:2 * NE * (l + 1), i, :], I[name].rearrange("e (h p) -> (e h) p", p=P)).then_inc(s["ld_bn"], 16)
            sp.dma_start(w1m, I["L0_mix_w1"].rearrange("(k p) n -> p k n", p=P)).then_inc(s["ld_small"], 16)
            sp.dma_start(rl[:, 0:KT, :], I["L0_ffn_Wr"].rearrange("(k p) e -> p k e", p=P)).then_inc(s["ld_small"], 16)
            for r in range(3):
                sp.dma_start(tmp[r * NE:(r + 1) * NE, 2, 0:D], I["L0_ffn_bo"]).then_inc(s["ld_small"], 16)
            sp.dma_start(b2bc[:, :], I["L0_mix_b2"].partition_broadcast(P)).then_inc(s["ld_small"], 16)
            sp.dma_start(brbc[:, :], I["L0_ffn_br"].partition_broadcast(P)).then_inc(s["ld_small"], 16)
            sp.dma_start(gkb[:, :], I["L0_mix_kln_g"].partition_broadcast(P)).then_inc(s["ld_small"], 16)
            sp.dma_start(bkb[:, :], I["L0_mix_kln_b"].partition_broadcast(P)).then_inc(s["ld_small"], 16)
            for r in range(P // HC):
                rows = slice(r * HC, (r + 1) * HC)
                sp.dma_start(gvc[rows, :], I["L0_mix_vln_g"].unsqueeze(1)).then_inc(s["ld_small"], 16)
                sp.dma_start(bvc[rows, :], I["L0_mix_vln_b"].unsqueeze(1)).then_inc(s["ld_small"], 16)
                for k in range(KT):
                    head = k * (P // HC) + r
                    sp.dma_start(bqc[rows, k:k + 1],
                                 I["L0_mix_b_qkv"][head * 3 * HC:head * 3 * HC + HC].unsqueeze(1)).then_inc(s["ld_small"], 16)
            for k in range(KT):
                sp.dma_start(b1c[:, k:k + 1], I["L0_mix_b1"][k * P:(k + 1) * P].unsqueeze(1)).then_inc(s["ld_small"], 16)

            need(sp, s["set_dve"], SETUP_A)
            def chunk_a(ch, e):
                if e is not None:
                    need(sp, s["wst_lo"], 3 * e)
                    for l, name in enumerate(("L0_ffn_W1", "L0_ffn_W2", "L0_ffn_Wo")):
                        src = I[name][bass.ds(e, 1), :, :].rearrange("e (k p) n -> p (e k) n", p=P)
                        sp.dma_start(wst[:, l, :].rearrange("p (k n) -> p k n", k=KT), src).then_inc(s["wst_ld"], 16)
                if not (isinstance(ch.c, int) and ch.c + 2 > NFULL):
                    if isinstance(ch.c, int):
                        nn = chunk(ch.c + 2)
                    else:
                        nn = Chunk(ch.c + 2, ch.half + 1, ch.par)
                    load_x(nn, s_x, (s["xnorm"], TPC * (ch.c + 1)))
                for t in range(ch.nt):
                    g = TPC * ch.c + t
                    tp = ch.tp
                    need(sp, s["xte"], g + 1)
                    sp.dma_start(tab_d[bass.ds(g * P, tp), :], xte[0:tp, t % 2, 0:TAB]).then_inc(s_tab[t % 2], 16)
                    sp.dma_start(al_d[bass.ds(g * P, tp), :], xte[0:tp, t % 2, TAB:XTW]).then_inc(s_tab[t % 2], 16)
            phase_a_loop(sp, chunk_a, ahead=2)

            need(sp, s["wst_lo"], 3 * NE)
            sp.dma_start(wst[:, 0, :].rearrange("p (k n) -> p k n", k=KT),
                         I["L0_mix_w2"].rearrange("(k p) n -> p k n", p=P)).then_inc(s["ld_stage"], 16)

            def load_idx(ch):
                need(sp, s["gath"], 2 * TPC * 16 * ch.c, alone=s["passed_sp"])
                rows = bass.ds(ch.c * CH, ch.rows)
                for a, name in enumerate(("dst", "src")):
                    sp.dma_start(idx[0:ch.tp, a, 0:ch.nt], I[name][rows].rearrange("(t p) -> p t", p=ch.tp),
                                 allow_slow_non_contiguous=True).then_inc(s["idx"], 16)

            def loads_b(ch):
                need(sp, s["fxn"], ch.c - 1)
                load_x(ch, s_xB, None)
                load_idx(ch)

            def store(ch):
                need(sp, s["acc"], 2 * NE * (ch.c + 1) if not ch.last else 2 * NE * NFULL + NE)
                sp.dma_start(ch.rows_of(out), acc[0:ch.tp, ch.par, 0:ch.nt, :]).then_inc(s_out[ch.par], 16)

            need(sp, s["xnorm"], NTILES)
            loads_b(chunk(0))
            loads_b(chunk(1))

            def chunk_b(ch):
                if not (isinstance(ch.c, int) and ch.c == 0):
                    store(ch.prev())
                if not (isinstance(ch.c, int) and ch.c + 2 > NFULL):
                    loads_b(chunk(ch.c + 2) if isinstance(ch.c, int) else Chunk(ch.c + 2, ch.half + 1, ch.par))
            phase_b_loop(sp, chunk_b, ahead=2)
            store(LAST)
            need(sp, s_out[0], 16 * (NFULL // 2 + 1))
            need(sp, s_out[1], 16 * (NFULL // 2))

        @block.gpsimd
        def _(pool):
            nc.gpsimd.memset(ident[:, :], 0.0).then_inc(s["id"], 1)
            nc.gpsimd.memset(onesf[:, :], 1.0).then_inc(s["ones"], 1)
            nc.gpsimd.memset(epsc[:, 0:1], LN_EPS).then_inc(s["eps"], 1)
            nc.gpsimd.memset(epsc[:, 1:2], BN_EPS).then_inc(s["eps"], 1)
            nc.gpsimd.memset(mhalf[:, :], -0.5).then_inc(s["ones"], 1)
            nc.gpsimd.memset(kvsum, 0.0).then_inc(s["ksum"], 1)
            nc.gpsimd.memset(kvT, 0.0).then_inc(s["ones"], 1)
            nc.gpsimd.memset(w3[:, :, :], 0.0).then_inc(s["ones"], 1)
            pool.wait_ge(s["id"], 1)
            nc.gpsimd.affine_select(out=ident[:, :], in_=ident[:, :], compare_op=ALU.not_equal, fill=1.0, base=0,
                                    pattern=[[-1, P]], channel_multiplier=1).then_inc(s["id"], 1)
            pool.wait_ge(s["ones"], 2)
            pch = Chain(pool, s["set_pool"])

            def keep_scalars(ch):
                need(pool, s["rstd"], ch.c + 1, alone=s["passed_pool"])
                cols = bass.ds(TPC * ch.c, ch.nt)
                nc.gpsimd.tensor_copy(rsA[0:ch.tp, cols], rs[0:ch.tp, ch.par, 0:ch.nt]).then_inc(s["rsl"], 1)
                nc.gpsimd.tensor_copy(nmA[0:ch.tp, cols], nm[0:ch.tp, ch.par, 0:ch.nt]).then_inc(s["rsl"], 1)

            keep_scalars(chunk(0))
            pool.wait_ge(s["ld_bn"], 16 * 10)
            b, g, be, m, v = (bnr[:, i, :] for i in range(5))
            pool.wait_ge(s["bn_rc"], 1)
            pch.step(nc.gpsimd.tensor_tensor(g, g, v, ALU.mult))
            pch.step(nc.gpsimd.tensor_tensor(b, b, m, ALU.subtract))
            pch.step(nc.gpsimd.tensor_tensor(b, b, g, ALU.mult))
            pch.step(nc.gpsimd.tensor_tensor(b, b, be, ALU.add))

            def chunk_a(ch, e):
                tp = ch.tp
                for t in range(ch.nt):
                    g = TPC * ch.c + t
                    p = t % 2
                    need(pool, s["kvn"], g + 1, alone=s["passed_pool"])
                    need(pool, s["ksum"], g + 1, alone=s["passed_pool"])
                    nc.gpsimd.tensor_tensor(G[0:tp, 0:2 * D], G[0:tp, 0:2 * D], kvn[0:tp, p, :], ALU.add).then_inc(s["ksum"], 1)
                    if e is not None and t < 3:
                        need(pool, s["wst_hi"], 3 * e + t + 1, alone=s["passed_pool"])
                        nc.gpsimd.tensor_tensor(wlo[:, bass.ds(e + t * NE, 1), :].rearrange("p a n -> p (a n)"), wst[:, t, :],
                                                whi[:, bass.ds(e + t * NE, 1), :].rearrange("p a n -> p (a n)").bitcast(fp32),
                                                ALU.subtract).then_inc(s["wst_lo"], 1)
                    if t == 2:
                        keep_scalars(ch.next())
            phase_a_loop(pool, chunk_a)

            pool.wait_ge(s["rsl"], 2 * (NFULL + 1))
            pool.wait_ge(s["xnorm"], NTILES)
            pool.wait_ge(s_tab[0], 32 * (2 * NFULL + 1))
            pool.wait_ge(s_tab[1], 32 * 2 * NFULL)
            pool.wait_ge(s["mid_pe"], 1)

            def gather(ch):
                need(pool, s["idx"], 32 * (ch.c + 1), alone=s["passed_pool"])
                for t in range(ch.nt):
                    nc.gpsimd.indirect_dma_start(G[0:ch.tp, t * TAB:(t + 1) * TAB], None, tab_d,
                                                 bass.IndirectOffsetOnAxis(ap=idx[0:ch.tp, 0, t:t + 1], axis=0)).then_inc(s["gath"], 16)
                    nc.gpsimd.indirect_dma_start(gal[0:ch.tp, t * GH:(t + 1) * GH], None, al_d,
                                                 bass.IndirectOffsetOnAxis(ap=idx[0:ch.tp, 1, t:t + 1], axis=0)).then_inc(s["gath"], 16)

            def scalars(ch):
                tp, nt = ch.tp, ch.nt
                need(pool, s["fxn"], ch.c, alone=s["passed_pool"])
                cols = bass.ds(TPC * ch.c, nt)
                nc.gpsimd.tensor_copy(rs[0:tp, 0, 0:nt], rsA[0:tp, cols]).then_inc(s["rsl"], 1)
                nc.gpsimd.tensor_copy(nm[0:tp, 0, 0:nt], nmA[0:tp, cols]).then_inc(s["rsl"], 1)
                need(pool, s["rsl"], 2 * (NFULL + 1) + 3 * ch.c + 1, alone=s["passed_pool"])
                nc.gpsimd.tensor_scalar(rs1[0:tp, 0:nt], rs[0:tp, 0, 0:nt], 1.0, 1.0, ALU.mult, ALU.add).then_inc(s["rsl"], 1)

            def front(ch, last=False):
                tp, nt = ch.tp, ch.nt
                b = 7 * ch.c
                gb = Chain(pool, s["gbase"], b, alone=s["passed_pool"])
                need(pool, s["fxn"], ch.c + 1, alone=s["passed_pool"])
                gb.step(nc.gpsimd.tensor_tensor(base[0:tp, 0:nt, :], base[0:tp, 0:nt, :],
                                                b2bc[0:tp, :].unsqueeze(1).broadcast_to([tp, nt, D]), ALU.add))
                need(pool, s["galpha"], ch.c + 1, alone=s["passed_pool"])
                heads = Gt[0:tp, 0:nt, 0:D].rearrange("p t (h d) -> p t h d", h=GH)
                gb.step(nc.gpsimd.tensor_tensor(heads, heads, wide(ga[0:tp, 0:nt, :], [tp, nt, GH, GC]), ALU.mult))
                gb.step(nc.gpsimd.tensor_tensor(heads[:, :, 0:2, :], heads[:, :, 0:2, :], heads[:, :, 2:4, :], ALU.add))
                gb.step(nc.gpsimd.tensor_tensor(heads[:, :, 0, :], heads[:, :, 0, :], heads[:, :, 1, :], ALU.add))
                bh = base[0:tp, 0:nt, :].rearrange("p t (h d) -> p t h d", h=GH)
                gb.step(nc.gpsimd.tensor_tensor(bh, bh, heads[:, :, 0, :].unsqueeze(2).broadcast_to([tp, nt, GH, GC]), ALU.add))
                if not last:
                    gather(ch.next())
                    scalars(ch.next())
                need(pool, s["fst"], ch.c + 1, alone=s["passed_pool"])
                gb.step(nc.gpsimd.tensor_scalar(rs[0:tp, 1, 0:nt], mv[0:tp, 0:nt, 1], 1.0, LN_EPS, ALU.mult, ALU.add))
                gb.step(nc.gpsimd.tensor_tensor(rs[0:tp, 1, 0:nt], rs[0:tp, 1, 0:nt], mhalf[0:tp, 0:nt], ALU.pow))
                nc.gpsimd.tensor_tensor(nm[0:tp, 1, 0:nt], mv[0:tp, 0:nt, 0], rs[0:tp, 1, 0:nt], ALU.mult).then_inc(s["frs"], 1)
                assert gb.n == 7

            scalars(chunk(0))
            gather(chunk(0))
            front(chunk(0))
            phase_b_loop(pool, lambda ch: None if ch.last else front(ch.next(), last=ch.next().last), ahead=2)

        @block.scalar
        def _(act):
            def copy(dst, src):
                return nc.scalar.activation(dst, src, ACT.Copy)

            act.wait_ge(s["ones"], 1)
            copy(onesr[:, :], onesf[:, :]).then_inc(s["set_act"], 1)

            act.wait_ge(s["eps"], 2)
            act.wait_ge(s["ld_bn"], 16 * 10)
            nc.scalar.activation(bnr[:, 4, :], bnr[:, 4, :], ACT.Sqrt, bias=epsc[0:4 * NE, 1:2]).then_inc(s["bn_sq"], 1)

            def x_sd(ch):
                need(act, s["stat"], TPC * ch.c + ch.nt)
                if not (isinstance(ch.c, int) and ch.c < 2):
                    need(act, s["xnorm"], TPC * (ch.c - 1))
                    need(act, s["rsl"], 2 * (ch.c - 1))
                nc.scalar.activation(rs[0:ch.tp, ch.par, 0:ch.nt], mv[0:ch.tp, 0:ch.nt, 1], ACT.Sqrt,
                                     bias=epsc[0:ch.tp, 0:1]).then_inc(s["xsd"], 1)

            def xnormed(ch, t):
                g = TPC * ch.c + t
                tp = ch.tp
                need(act, s["rstd"], ch.c + 1)
                need(act, s["tr"], g - 1)
                nc.scalar.activation(xn[0:tp, t % 2, :], xb[0:tp, ch.par, t, :], ACT.Identity,
                                     bias=nm[0:tp, ch.par, t:t + 1], scale=rs[0:tp, ch.par, t:t + 1]).then_inc(s["xnorm"], 1)

            def t_hi(ch, t):
                g = TPC * ch.c + t
                need(act, s["tr"], g + 1)
                if not (isinstance(ch.c, int) and ch.c < 2):
                    need(act, s["xt"], TPC * (ch.c - 1))
                cols = slice(t * P, t * P + ch.tp)
                src = Tb[t % 2][:, 0:KT * P].rearrange("p (k r) -> p k r", k=KT)[:, :, 0:ch.tp]
                copy(xTh[:, ch.par, :, cols], src).then_inc(s["thi"], 1)

            def kv_sd(g, p, tp):
                need(act, s["ssum"], g + 1)
                need(act, s["kvn"], g - 1)
                nc.scalar.activation(rk[0:tp, p, :], ss[0:tp, p, :], ACT.Sqrt, bias=epsc[0:tp, 0:1],
                                     scale=1.0 / HC).then_inc(s["krs"], 1)

            def kv_hi(g, p, tp):
                need(act, s["kvn"], g + 1)
                need(act, s["S"], g - 1)
                copy(kvh[0:tp, p, :], kvn[0:tp, p, :]).then_inc(s["kvhi"], 1)

            x_sd(chunk(0))
            for t in (0, 1):
                xnormed(chunk(0), t)
            for t in range(TPC):
                t_hi(chunk(0), t)
                if t + 2 < TPC:
                    xnormed(chunk(0), t + 2)

            def chunk_a(ch, e):
                tp = ch.tp
                for t in range(ch.nt):
                    g = TPC * ch.c + t
                    p = t % 2
                    if not (isinstance(ch.c, int) and g == 0):
                        kv_sd(g - 1, 1 - p, P)
                    for u in of_next(ch, t, TURN):
                        xnormed(ch.next(), u)
                    need(act, s["kv"], g + 1)
                    need(act, s["ssum"], g)
                    nc.scalar.activation(sq[0:tp, :], KVb[p][0:tp, :], ACT.Square).then_inc(s["sq"], 1)
                    need(act, s["xt"], g + 1)
                    need(act, s_tab[p], 32 * (2 * ch.c + t // 2))
                    copy(xte[0:tp, p, :], XTb[p][0:tp, 0:XTW]).then_inc(s["xte"], 1)
                    if not (isinstance(ch.c, int) and g == 0):
                        kv_hi(g - 1, 1 - p, P)
                    if t == 1:
                        x_sd(ch.next())
                    for u in of_next(ch, t, TURN):
                        t_hi(ch.next(), u)
                    if e is not None and t < 3:
                        if t == 0:
                            need(act, s["wst_ld"], 48 * (e + 1))
                        copy(whi[:, bass.ds(e + t * NE, 1), :].rearrange("p a n -> p (a n)"), wst[:, t, :]).then_inc(s["wst_hi"], 1)
            phase_a_loop(act, chunk_a)
            kv_sd(NTILES - 1, 0, TAIL)
            kv_hi(NTILES - 1, 0, TAIL)

            act.wait_ge(s["mid_dve"], MID)

            def relu(layer, ch, e, h, guard):
                psum, done = (L1b, s["r1"]) if layer == 0 else (L2b, s["r2"])
                need(act, s["l1"] if layer == 0 else s["l2"], 2 * NE * ch.c + 2 * e + h + 1)
                need(act, *guard)
                col = 2 * e + h
                nc.scalar.activation(tmp[:, h, 0:ch.rows], psum[h][:, 0:ch.rows], ACT.Relu,
                                     bias=bnp[:, 1, layer, col:col + 1],
                                     scale=bnp[:, 0, layer, col:col + 1]).then_inc(done, 1)

            def relu1(ch, e):
                for h in range(2):
                    before = 2 * NE * ch.c + 2 * (e - 2) + h + 1
                    if isinstance(ch.c, int) and ch.c == 0 and e == 1:
                        relu(0, ch, e, h, (s["h1"], h + 1))
                    else:
                        relu(0, ch, e, h, (s["h2"], before))

            def relu2(ch, e):
                for h in range(2):
                    if ch.last and e == NE - 1:
                        relu(1, ch, e, h, (s["h2"], 2 * NE * ch.c + 2 * (e - 1) + h + 1))
                    else:
                        relu(1, ch, e, h, (s["h1"], 2 * NE * ch.c + 2 * (e + 1) + h + 1))

            def front(ch, e):
                tp, nt, R = ch.tp, ch.nt, ch.rows
                if e == 1:
                    need(act, s["glog"], ch.c + 1)
                    nc.scalar.activation(ga[0:tp, 0:nt, :], ga[0:tp, 0:nt, :], ACT.Exp).then_inc(s["gexp"], 1)
                    for k in range(KT):
                        need(act, s["fT"], KT * ch.c + k + 1)
                        need(act, s["fm2"], 2 * ch.c)
                        copy(xmh[:, k, 0:R], Fb[k][:, 0:R]).then_inc(s["fThi"], 1)
                if e == 2:
                    for h in range(2):
                        need(act, s["fm1"], 2 * ch.c + h + 1)
                        need(act, s["fmh"], 4 * ch.c + 2 * h)
                        nc.scalar.activation(tmp[:, 2, 0:R], Fb[h][:, 0:R], ACT.Gelu, bias=c1c[:, h:h + 1]).then_inc(s["gelu"], 1)
                if e == 5:
                    for k in range(KT):
                        need(act, s["f2T"], KT * ch.c + k + 1)
                        need(act, s["l1"], 2 * NE * (ch.c - 1))
                        copy(xTh[:, ch.par, k, 0:R], Fb[k][:, 0:R]).then_inc(s["f2hi"], 1)
                if e == 6:
                    need(act, s["flg"], ch.c + 1)
                    nc.scalar.activation(rl[0:tp, 0:nt, :], rl[0:tp, 0:nt, :], ACT.Exp).then_inc(s["fex"], 1)
                if e == 7:
                    need(act, s["fw3T"], ch.c + 1)
                    need(act, s["fbo"], 2 * ch.c)
                    copy(w3T[:, 0:nt, 0:tp], Fb[1][:, 0:nt * P].rearrange("p (t r) -> p t r", r=P)[:, :, 0:tp]).then_inc(s["fw3c"], 1)

            for e in range(NE):
                front(chunk(0), e)
            relu1(chunk(0), 0)

            def chunk_b(ch):
                nxt = None if ch.last else ch.next()
                for e in range(NE):
                    if e + 1 < NE:
                        relu1(ch, e + 1)
                    elif nxt is not None:
                        relu1(nxt, 0)
                    if nxt is not None:
                        front(nxt, e)
                    relu2(ch, e)
            phase_b_loop(act, chunk_b)

        @block.tensor
        def _(pe):
            pe.wait_ge(s["id"], 2)

            def transposes(ch, t):
                g = TPC * ch.c + t
                need(pe, s["xnorm"], g + 1)
                need(pe, s["tlo"], g - 1)
                for k in range(KT):
                    last = nc.tensor.transpose(Tb[t % 2][:, k * P:k * P + ch.tp], xn[0:ch.tp, t % 2, k * P:(k + 1) * P],
                                               ident[0:ch.tp, 0:ch.tp])
                last.then_inc(s["tr"], 1)

            for t in range(TPC):
                transposes(chunk(0), t)
            pe.wait_ge(s["set_pool"], 4)
            for i, row in enumerate((1, 0)):
                last = nc.tensor.transpose(Sb[0][:, i * 4 * NE:(i + 1) * 4 * NE], bnr[:, row, :], ident[0:4 * NE, 0:4 * NE])
            last.then_inc(s["bn_t"], 1)
            pe.wait_ge(s["set_dve"], SETUP_Q)
            for k in range(KT):
                for g in range(2):
                    last = nc.tensor.transpose(Sb[1][:, g * D + k * P:g * D + (k + 1) * P],
                                               Pm[:, k, g * P:(g + 1) * P], ident[:, :])
            last.then_inc(s["wq_t"], 1)
            pe.wait_ge(s["set_act"], 1)
            pe.wait_ge(s["set_dve"], SETUP_ALL)
            pe.wait_ge(s["wq_ev"], 2)

            def s_product(g, p, tp, first=False, final=False):
                need(pe, s["kvlo"], g + 1)
                for grp in range(2):
                    kc, vc = slice(grp * P, (grp + 1) * P), slice(D + grp * P, D + (grp + 1) * P)
                    dst = Sb[grp][:, 0:P]
                    nc.tensor.matmul(dst, kvh[0:tp, p, vc], kvh[0:tp, p, kc], start=first, stop=False, skip_group_check=True)
                    nc.tensor.matmul(dst, kvh[0:tp, p, vc], kvl[0:tp, p, kc], start=False, stop=False, skip_group_check=True)
                    last = nc.tensor.matmul(dst, kvl[0:tp, p, vc], kvh[0:tp, p, kc], start=False, stop=final, skip_group_check=True)
                last.then_inc(s["S"], 1)

            def chunk_a(ch, e):
                tp = ch.tp
                for t in range(ch.nt):
                    g = TPC * ch.c + t
                    p = t % 2
                    cols = slice(t * P, t * P + tp)
                    lhs = [(xTh[:, ch.par, k, cols], xTl[:, ch.par, k, cols]) for k in range(KT)]
                    need(pe, s["tlo"], g + 1)
                    need(pe, s["kvn"], g - 1)
                    nc.tensor.matmul(KVb[p][0:tp, :], onesr[:, 0:tp], brow[:, :], start=True, stop=False)
                    mm3(KVb[p][0:tp, :], lhs, [(wAh[:, k, 0:2 * D], wAl[:, k, 0:2 * D]) for k in range(KT)],
                        lead=True).then_inc(s["kv"], 1)
                    need(pe, s["xte"], g - 1)
                    mm3(XTb[p][0:tp, 0:XTW], lhs, [(wAh[:, k, 2 * D:WA], wAl[:, k, 2 * D:WA]) for k in range(KT)]).then_inc(s["xt"], 1)
                    for u in of_next(ch, t, TURN):
                        transposes(ch.next(), u)
                    if not (isinstance(ch.c, int) and g < 2):
                        s_product(g - 2, p, P, first=isinstance(ch.c, int) and g == 2)
            phase_a_loop(pe, chunk_a)
            s_product(NTILES - 2, 1, P)
            s_product(NTILES - 1, 0, TAIL, final=True)

            pe.wait_ge(s["ksum"], NTILES + 1)
            pe.wait_ge(s["kvn"], NTILES)
            pe.wait_ge(s["xte"], NTILES)
            nc.tensor.matmul(KVb[0][:, 0:D], onesf[:, :], kvsum[:, 0:D], start=True, stop=True)
            for grp in range(2):
                last = nc.tensor.matmul(KVb[1][:, grp:grp + 1], kvsum[:, D + grp * P:D + (grp + 1) * P], onesf[:, 0:1],
                                        start=True, stop=True)
            last.then_inc(s["mid_pe"], 1)
            pe.wait_ge(s["mid_dve"], MID_KV)
            for grp in range(2):
                last = nc.tensor.matmul(XTb[0][:, grp * D:(grp + 1) * D], kvT[:, grp, :], w1m[:, grp, :], start=True, stop=True)
            last.then_inc(s["mid_pe"], 1)
            pe.wait_ge(s["mid_dve"], MID_P)
            for k in range(KT):
                for grp in range(2):
                    last = nc.tensor.matmul(KVb[0][:, k * D:(k + 1) * D], wqT[:, grp, k * P:(k + 1) * P], Pm[:, grp, :],
                                            start=(grp == 0), stop=(grp == 1))
            last.then_inc(s["mid_pe"], 1)
            for h in range(2):
                for grp in range(2):
                    last = nc.tensor.matmul(KVb[1][:, 8 + h:9 + h], Pm[:, grp, h * P:(h + 1) * P], bqc[:, grp:grp + 1],
                                            start=(grp == 0), stop=(grp == 1))
            last.then_inc(s["mid_pe"], 1)
            pe.wait_ge(s["mid_dve"], MID)

            def W(layer, e, k, lo, hi):
                m = layer * NE + e
                return whi[:, m, k * D + lo:k * D + hi], wlo[:, m, k * D + lo:k * D + hi]

            def L1(ch, e):
                R = ch.rows
                if e == 0:
                    need(pe, s["f2lo"], KT * (ch.c + 1))
                for h in range(2):
                    need(pe, s["r1"], 2 * NE * ch.c + 2 * (e - 1) + h + 1)
                    mm3(L1b[h][:, 0:R], [W(0, e, k, h * P, (h + 1) * P) for k in range(KT)],
                        [(xTh[:, ch.par, k, 0:R], xTl[:, ch.par, k, 0:R]) for k in range(KT)]).then_inc(s["l1"], 1)

            def L2(ch, e):
                R = ch.rows
                for h in range(2):
                    need(pe, s["r2"], 2 * NE * ch.c + 2 * (e - 1) + h + 1)
                    if h == 0:
                        need(pe, s["h1"], 2 * NE * ch.c + 2 * e + 2)
                    mm3(L2b[h][:, 0:R], [W(1, e, k, h * P, (h + 1) * P) for k in range(KT)],
                        [(h1h[:, e % 2, k, 0:R], h1l[:, e % 2, k, 0:R]) for k in range(KT)]).then_inc(s["l2"], 1)

            def L3(ch, e):
                tp = ch.tp
                need(pe, s["h2"], 2 * NE * ch.c + 2 * e + 2)
                nb = (ch.nt + 1) // 2
                for b in range(nb):
                    need(pe, s["acc"], 2 * NE * ch.c + (nb * (e - 1) + b + 1 if ch.last and e > 0 else 2 * (e - 1) + b + 1))
                    for t in range(2 * b, min(2 * b + 2, ch.nt)):
                        cols = slice(t * P, t * P + tp)
                        last = mm3(Yb[b][0:tp, (t % 2) * D:(t % 2 + 1) * D],
                                   [(h2h[:, k, cols], h2l[:, k, cols]) for k in range(KT)], [W(2, e, k, 0, D) for k in range(KT)])
                    last.then_inc(s["y"], 1)

            def turned(ch, src):
                for k in range(KT):
                    for t in range(ch.nt):
                        last = nc.tensor.transpose(Fb[k][:, t * P:t * P + ch.tp], src[0:ch.tp, t, k * P:(k + 1) * P],
                                                   ident[0:ch.tp, 0:ch.tp])
                    yield last

            def front(ch, e, end=False):
                tp, nt, R = ch.tp, ch.nt, ch.rows
                nb = (nt + 1) // 2
                if e == 1:
                    need(pe, s["fxn"], ch.c + 1)
                    need(pe, s["fai"], 2 * ch.c)
                    for last in turned(ch, xn):
                        last.then_inc(s["fT"], 1)
                if e == 2:
                    need(pe, s["fTlo"], KT * (ch.c + 1))
                    for h in range(2):
                        mm3(Fb[h][:, 0:R], [(mwh[:, 0, k, h * P:(h + 1) * P], mwl[:, 0, k, h * P:(h + 1) * P]) for k in range(KT)],
                            [(xmh[:, k, 0:R], xml[:, k, 0:R]) for k in range(KT)]).then_inc(s["fm1"], 1)
                if e == 3:
                    need(pe, s["fmh"], 4 * (ch.c + 1))
                    for b in range(nb):
                        for t in range(2 * b, min(2 * b + 2, nt)):
                            cols = slice(t * P, t * P + tp)
                            last = mm3(Fb[b][0:tp, (t % 2) * D:(t % 2 + 1) * D],
                                       [(hmh[:, k, cols], hml[:, k, cols]) for k in range(KT)],
                                       [(mwh[:, 1, k, :], mwl[:, 1, k, :]) for k in range(KT)])
                        last.then_inc(s["fm2"], 1)
                if e == 5:
                    need(pe, s["fx2n"], ch.c + 1)
                    for last in turned(ch, xn):
                        last.then_inc(s["f2T"], 1)
                if e == 6:
                    need(pe, s["f2lo"], KT * (ch.c + 1))
                    for t in range(nt):
                        cols = slice(t * P, t * P + tp)
                        last = mm3(Fb[0][0:tp, t * NE:(t + 1) * NE],
                                   [(xTh[:, ch.par, k, cols], xTl[:, ch.par, k, cols]) for k in range(KT)],
                                   [(wrh[:, k, :], wrl[:, k, :]) for k in range(KT)])
                    last.then_inc(s["frt"], 1)
                if e == 7 and not end:
                    need(pe, s["fw3"], ch.c + 1)
                    for t in range(nt):
                        last = nc.tensor.transpose(Fb[1][:, t * P:t * P + tp], w3[0:tp, t, :], ident[0:tp, 0:tp])
                    last.then_inc(s["fw3T"], 1)
                if e == 7 and end:
                    need(pe, s["fw3c"], ch.c + 1)
                    for b in range(nb):
                        for t in range(2 * b, min(2 * b + 2, nt)):
                            last = nc.tensor.matmul(Fb[b][0:tp, (t % 2) * D:(t % 2 + 1) * D], w3T[:, t, 0:tp], bo3[:, :],
                                                    start=True, stop=True)
                        last.then_inc(s["fbo"], 1)

            for e in range(NE):
                front(chunk(0), e)
            front(chunk(0), NE - 1, end=True)
            L1(chunk(0), 0)

            def chunk_b(ch):
                nxt = None if ch.last else ch.next()
                for e in range(NE):
                    if e + 1 < NE:
                        L1(ch, e + 1)
                    elif nxt is not None:
                        L1(nxt, 0)
                    if e > 0:
                        L3(ch, e - 1)
                    elif not (isinstance(ch.c, int) and ch.c == 0):
                        L3(ch.prev(), NE - 1)
                    if nxt is not None:
                        front(nxt, e)
                    L2(ch, e)
                if nxt is not None:
                    front(nxt, NE - 1, end=True)
            phase_b_loop(pe, chunk_b)
            L3(LAST, NE - 1)

        @block.vector
        def _(dve):
            V = nc.vector

            def copy(dst, src):
                return V.tensor_copy(dst, src)

            def low(dst, full, high):
                return V.tensor_tensor(dst, full, high.bitcast(fp32), ALU.subtract)

            def stats(ch, t, more=None):
                tp = ch.tp
                V.bn_stats(st6[0:tp, t, :], xb[0:tp, ch.par, t, :]).then_inc(s["dsm"], 1)

            def aggr(ch, t):
                V.bn_aggr(mv[0:ch.tp, t, :], st6[0:ch.tp, t, :]).then_inc(s["stat"], 1)

            def x_rstd(ch):
                tp, nt = ch.tp, ch.nt
                need(dve, s["xsd"], ch.c + 1)
                r, m = rs[0:tp, ch.par, 0:nt], nm[0:tp, ch.par, 0:nt]
                V.reciprocal(r, r).then_inc(s["xrec"], 1)
                need(dve, s["xrec"], ch.c + 1, alone=s["passed_dve"])
                V.scalar_tensor_tensor(m, mv[0:tp, 0:nt, 0], -1.0, r, ALU.mult, ALU.mult).then_inc(s["rstd"], 1)

            def t_lo(ch, t):
                g = TPC * ch.c + t
                need(dve, s["thi"], g + 1)
                cols = slice(t * P, t * P + ch.tp)
                src = Tb[t % 2][:, 0:KT * P].rearrange("p (k r) -> p k r", k=KT)[:, :, 0:ch.tp]
                low(xTl[:, ch.par, :, cols], src, xTh[:, ch.par, :, cols]).then_inc(s["tlo"], 1)

            def kv_lo(g, p, tp):
                need(dve, s["kvhi"], g + 1)
                low(kvl[0:tp, p, :], kvn[0:tp, p, :], kvh[0:tp, p, :]).then_inc(s["kvlo"], 1)

            def kv_norm(g, p, tp):
                need(dve, s["krs"], g + 1)
                V.reciprocal(rk[0:tp, p, :], rk[0:tp, p, :]).then_inc(s["krec"], 1)
                need(dve, s["krec"], g + 1)
                need(dve, s["ksum"], g)
                need(dve, s["kvhi"], g - 1)
                V.tensor_tensor(kvn[0:tp, p, :].rearrange("p (h d) -> p h d", h=NG),
                                KVb[p][0:tp, :].rearrange("p (h d) -> p h d", h=NG),
                                wide(rk[0:tp, p, :], [tp, NG, HC]), ALU.mult).then_inc(s["kvn"], 1)

            def stats_of(ch, tiles):
                need(dve, s_x[ch.par], 16 * (ch.half + 1))
                if not (isinstance(ch.c, int) and ch.c == 0):
                    need(dve, s["xsd"], ch.c)
                for t in tiles:
                    stats(ch, t)
                for t in tiles:
                    need(dve, s["dsm"], TPC * ch.c + tiles[-1] + 1, alone=s["passed_dve"])
                    aggr(ch, t)

            stats_of(chunk(0), range(TPC))
            cc = Chain(dve, s["set_dve"])
            cc.step(V.memset(brow[:, :].bitcast(fp32), 0.0))
            cc.step(V.memset(bo3[:, :].bitcast(fp32), 0.0))
            x_rstd(chunk(0))
            dve.wait_ge(s["bn_sq"], 1)
            V.reciprocal(bnr[:, 4, :], bnr[:, 4, :]).then_inc(s["bn_rc"], 1)
            dve.wait_ge(s["ld_w"], 16 * 5)
            wf = wst[:, 2, :]
            def centred(src4, rows, dst_hi, dst_lo):
                for i in range(2):
                    part = src4[:, :, (i + 1) * HC:(i + 2) * HC]
                    m8 = mn[0:rows, i * NH:(i + 1) * NH]
                    cc.step(V.tensor_reduce(m8, part, AX.X, ALU.add))
                    cc.step(V.tensor_scalar(m8, m8, 1.0 / HC, None, ALU.mult))
                    w3d = wf[0:rows, i * D:(i + 1) * D].rearrange("p (h d) -> p h d", h=NH)
                    cc.step(V.tensor_tensor(w3d, part, wide(m8, [rows, NH, HC]), ALU.subtract))
                cc.step(copy(dst_hi, wf[0:rows, 0:2 * D]))
                if dst_lo is not None:
                    cc.step(low(dst_lo, wf[0:rows, 0:2 * D], dst_hi))
            for k in range(KT):
                centred(wqkv[:, k, :].rearrange("p (h c) -> p h c", h=NH), P, wAh[:, k, 0:2 * D], wAl[:, k, 0:2 * D])
            b4 = tmp[0:2, 0:2, :].rearrange("p a b -> p (a b)")[:, 0:3 * D].rearrange("p (h c) -> p h c", h=NH)
            centred(b4, 2, brow[0:2, :], None)
            cc.step(low(tmp[0:2, 0, :], wf[0:2, 0:2 * D], brow[0:2, :]))
            cc.step(copy(brow[0:2, :], tmp[0:2, 0, :]))
            cc.step(copy(brow[0:1, :], wf[0:1, 0:2 * D]))
            for k in range(KT):
                wk = wst[:, 0, k * D:(k + 1) * D]
                cc.step(copy(wf[:, 0:D], wk))
                for i in range(2):
                    cc.step(V.tensor_tensor(tmp[:, 0, 0:D], wk, wst[:, 1, i * D:(i + 1) * D], ALU.mult))
                    cc.step(V.tensor_reduce(wf[:, D + i * GH:D + (i + 1) * GH],
                                            tmp[:, 0, 0:D].rearrange("p (h d) -> p h d", h=GH), AX.X, ALU.add))
                cc.step(copy(wAh[:, k, 2 * D:WA], wf[:, 0:XTW]))
                cc.step(low(wAl[:, k, 2 * D:WA], wf[:, 0:XTW], wAh[:, k, 2 * D:WA]))
            assert cc.n == SETUP_A
            for t in range(TPC):
                t_lo(chunk(0), t)
            for k in range(KT):
                cc.step(copy(Pm[:, k, :].rearrange("p (h d) -> p h d", h=NH),
                             wqkv[:, k, :].rearrange("p (h c) -> p h c", h=NH)[:, :, 0:HC]))
            assert cc.n == SETUP_Q
            dve.wait_ge(s["ld_small"], 16 * LD_SMALL)
            cc.step(copy(wrh[:, :, :], rl[:, 0:KT, :]))
            cc.step(low(wrl[:, :, :], rl[:, 0:KT, :], wrh[:, :, :]))
            bo = tmp[0:3 * NE, 2, 0:D]
            cc.step(copy(bo3[0:3 * NE, :], bo))
            cc.step(low(tmp[0:3 * NE, 1, 0:D], bo, bo3[0:3 * NE, :]))
            cc.step(copy(bo3[0:3 * NE, :], tmp[0:3 * NE, 1, 0:D]))
            cc.step(copy(bo3[0:2 * NE, :], tmp[0:2 * NE, 2, 0:D]))
            assert cc.n == SETUP_ALL
            dve.wait_ge(s["bn_t"], 1)
            copy(bnp[:, :, :, :].rearrange("p a l b -> p (a l b)"), Sb[0][:, 0:8 * NE]).then_inc(s["wq_ev"], 1)
            dve.wait_ge(s["wq_t"], 1)
            copy(wqT.rearrange("p a b -> p (a b)"), Sb[1][:, :]).then_inc(s["wq_ev"], 1)

            def chunk_a(ch, e):
                tp = ch.tp
                for t in range(ch.nt):
                    g = TPC * ch.c + t
                    p = t % 2
                    if not (isinstance(ch.c, int) and g == 0):
                        kv_norm(g - 1, 1 - p, P)
                    tiles = of_next(ch, t, STAT_TURN)
                    if tiles:
                        stats_of(ch.next(), tiles)
                    need(dve, s["sq"], g + 1)
                    need(dve, s["krs"], g - 1)
                    V.tensor_reduce(ss[0:tp, p, :], sq[0:tp, :].rearrange("p (h d) -> p h d", h=NG), AX.X, ALU.add).then_inc(s["ssum"], 1)
                    if not (isinstance(ch.c, int) and g == 0):
                        kv_lo(g - 1, 1 - p, P)
                    if t == 1:
                        x_rstd(ch.next())
                    for u in of_next(ch, t, TURN):
                        t_lo(ch.next(), u)
            phase_a_loop(dve, chunk_a)
            kv_norm(NTILES - 1, 0, TAIL)
            kv_lo(NTILES - 1, 0, TAIL)

            md = Chain(dve, s["mid_dve"])
            dve.wait_ge(s["S"], NTILES)
            dve.wait_ge(s["mid_pe"], 1)
            dve.wait_ge(s["ones"], 4)
            sv = mn[:, 0:2]
            md.step(copy(sv, KVb[1][:, 0:2]))
            t1, t2 = tmp[:, 0, 0:P], tmp[:, 1, 0:P]
            four = [P, P // HC, HC]
            gk4 = gkb[:, :].unsqueeze(1).broadcast_to(four)
            bk4 = bkb[:, :].unsqueeze(1).broadcast_to(four)
            def v4(ap):
                return ap.rearrange("p (h d) -> p h d", d=HC)
            for grp in range(2):
                md.step(V.tensor_tensor(v4(t1), v4(Sb[grp][:, 0:P]), gk4, ALU.mult))
                md.step(V.tensor_scalar(v4(t2), bk4, sv[:, grp:grp + 1], None, ALU.mult))
                md.step(V.tensor_tensor(t1, t1, t2, ALU.add))
                md.step(V.tensor_scalar(t1, t1, gvc[:, :], None, ALU.mult))
                md.step(V.tensor_tensor(v4(t2), v4(KVb[0][:, grp * P:(grp + 1) * P]), gk4, ALU.mult))
                md.step(V.scalar_tensor_tensor(v4(t2), bk4, float(N), v4(t2), ALU.mult, ALU.add))
                md.step(V.scalar_tensor_tensor(t1, t2, bvc[:, :], t1, ALU.mult, ALU.add))
                for h in range(P // HC):
                    b = slice(h * HC, (h + 1) * HC)
                    md.step(V.tensor_scalar(kvT[b, grp, b], tmp[b, 0, b], 1.0 / N, None, ALU.mult))
            assert md.n == MID_KV
            dve.wait_ge(s["mid_pe"], 2)
            md.step(copy(Pm.rearrange("p a b -> p (a b)"), XTb[0][:, :]))
            assert md.n == MID_P
            dve.wait_ge(s["mid_pe"], 3)
            Mf = tmp[:, 0, :]
            md.step(V.tensor_tensor(Mf, KVb[0][:, :], w1m.rearrange("p a b -> p (a b)"), ALU.add))
            mh, ml = (m[:, 0, :, :].rearrange("p a b -> p (a b)") for m in (mwh, mwl))
            md.step(copy(mh, Mf))
            md.step(low(ml, Mf, mh))
            dve.wait_ge(s["ld_stage"], 16)
            mh, ml = (m[:, 1, :, :].rearrange("p a b -> p (a b)") for m in (mwh, mwl))
            md.step(copy(mh, wst[:, 0, :]))
            md.step(low(ml, wst[:, 0, :], mh))
            dve.wait_ge(s["mid_pe"], 4)
            md.step(V.tensor_tensor(c1c[:, :], KVb[1][:, 8:10], b1c[:, :], ALU.add))
            assert md.n == MID

            def hid1(ch, e):
                R = ch.rows
                for h in range(2):
                    n = 2 * NE * ch.c + 2 * e + h
                    need(dve, s["r1"], n + 1)
                    need(dve, s["l2"], 2 * NE * ch.c + 2 * (e - 2) + 2)
                    copy(h1h[:, e % 2, h, 0:R], tmp[:, h, 0:R]).then_inc(s["hi1"], 1)
                    dve.wait_ge(s["hi1"], n + 1)
                    low(h1l[:, e % 2, h, 0:R], tmp[:, h, 0:R], h1h[:, e % 2, h, 0:R]).then_inc(s["h1"], 1)

            def hid2(ch, e):
                R = ch.rows
                for h in range(2):
                    n = 2 * NE * ch.c + 2 * e + h
                    need(dve, s["r2"], n + 1)
                    need(dve, s["y"], 2 * NE * ch.c + (e if ch.last else 2 * e))
                    copy(h2h[:, h, 0:R], tmp[:, h, 0:R]).then_inc(s["hi2"], 1)
                    dve.wait_ge(s["hi2"], n + 1)
                    low(h2l[:, h, 0:R], tmp[:, h, 0:R], h2h[:, h, 0:R]).then_inc(s["h2"], 1)

            def accumulate(ch, e):
                tp, nt = ch.tp, ch.nt
                nb = (nt + 1) // 2
                need(dve, s["fai"], 2 * ch.c + nb)
                for b in range(nb):
                    n = 2 * NE * ch.c + nb * e + b
                    need(dve, s["y"], n + 1)
                    if e > 0:
                        need(dve, s["acc"], n + 1 - nb)
                    for t in range(2 * b, min(2 * b + 2, nt)):
                        a = acc[0:tp, ch.par, t, :]
                        last = V.scalar_tensor_tensor(a, Yb[b][0:tp, (t % 2) * D:(t % 2 + 1) * D], wts(ch)[0:tp, t, e:e + 1], a,
                                                      ALU.mult, ALU.add)
                    last.then_inc(s["acc"], 1)

            def wts(ch):
                return wpar[ch.par]

            def front(ch, e, end=False):
                tp, nt, R = ch.tp, ch.nt, ch.rows
                nb = (nt + 1) // 2
                sm = Chain(dve, s["dsm"], NTILES + PER * ch.c + OFF[e, end])
                if e == 0:
                    need(dve, s_xB[ch.par], 16 * (ch.half + 1))
                    need(dve, s["rsl"], 2 * (NFULL + 1) + 3 * (ch.c + 1))
                    need(dve, s["f2T"], KT * ch.c)
                    need(dve, s["gbase"], 7 * ch.c)
                    for t in range(nt):
                        V.tensor_scalar(xn[0:tp, t, :], xb[0:tp, ch.par, t, :], rs[0:tp, 0, t:t + 1], nm[0:tp, 0, t:t + 1],
                                        ALU.mult, ALU.add)
                        last = V.tensor_scalar(base[0:tp, t, :], xb[0:tp, ch.par, t, :], rs1[0:tp, t:t + 1], nm[0:tp, 0, t:t + 1],
                                               ALU.mult, ALU.add)
                    last.then_inc(s["fxn"], 1)
                    need(dve, s["gath"], 2 * TPC * 16 * ch.c + 2 * nt * 16)
                    a = ga[0:tp, 0:nt, :]
                    sm.step(V.tensor_tensor(a, Gt[0:tp, 0:nt, D:TAB], gal[0:tp, 0:nt * GH].rearrange("p (t h) -> p t h", h=GH), ALU.add))
                    sm.step(V.scalar_tensor_tensor(a, a, 0.01, a, ALU.mult, ALU.max))
                    sm.step(V.tensor_reduce(gs[0:tp, 0, 0:nt], a, AX.X, ALU.max))
                    V.tensor_tensor(a, a, wide(gs[0:tp, 0, 0:nt], [tp, nt, GH]), ALU.subtract).then_inc(s["glog"], 1)
                if e == 1:
                    need(dve, s["gexp"], ch.c + 1)
                    a = ga[0:tp, 0:nt, :]
                    sm.step(V.tensor_reduce(gs[0:tp, 1, 0:nt], a, AX.X, ALU.add))
                    sm.step(V.reciprocal(gs[0:tp, 0, 0:nt], gs[0:tp, 1, 0:nt]))
                    V.tensor_tensor(a, a, wide(gs[0:tp, 0, 0:nt], [tp, nt, GH]), ALU.mult).then_inc(s["galpha"], 1)
                    for k in range(KT):
                        need(dve, s["fThi"], KT * ch.c + k + 1)
                        low(xml[:, k, 0:R], Fb[k][:, 0:R], xmh[:, k, 0:R]).then_inc(s["fTlo"], 1)
                if e == 2:
                    for h in range(2):
                        n = 4 * ch.c + 2 * h
                        need(dve, s["gelu"], 2 * ch.c + h + 1)
                        need(dve, s["fm1"], 2 * ch.c + 2)
                        copy(hmh[:, h, 0:R], tmp[:, 2, 0:R]).then_inc(s["fmh"], 1)
                        dve.wait_ge(s["fmh"], n + 1)
                        low(hml[:, h, 0:R], tmp[:, 2, 0:R], hmh[:, h, 0:R]).then_inc(s["fmh"], 1)
                if e == 3:
                    need(dve, s["gbase"], 7 * ch.c + 5)
                    if not (isinstance(ch.c, int) and ch.c < 2):
                        need(dve, s_out[ch.par], 16 * ch.half)
                    for b in range(nb):
                        need(dve, s["fm2"], 2 * ch.c + b + 1)
                        ts = range(2 * b, min(2 * b + 2, nt))
                        t0, t1_ = ts[0], ts[-1] + 1
                        V.tensor_tensor(acc[0:tp, ch.par, t0:t1_, :],
                                        Fb[b][0:tp, 0:(t1_ - t0) * D].rearrange("p (t d) -> p t d", d=D),
                                        base[0:tp, t0:t1_, :], ALU.add).then_inc(s["fx2"], 1)
                    dve.wait_ge(s["fx2"], 2 * ch.c + nb)
                    for t in range(nt):
                        last = V.bn_stats(st6[0:tp, t, :], acc[0:tp, ch.par, t, :])
                    sm.step(last)
                    need(dve, s["frs"], ch.c, alone=s["passed_dve"])
                    for t in range(nt):
                        last = V.bn_aggr(mv[0:tp, t, :], st6[0:tp, t, :])
                    last.then_inc(s["fst"], 1)
                if e == 4:
                    need(dve, s["frs"], ch.c + 1)
                    need(dve, s["fT"], KT * (ch.c + 1))
                    for t in range(nt):
                        last = V.tensor_scalar(xn[0:tp, t, :], acc[0:tp, ch.par, t, :], rs[0:tp, 1, t:t + 1], nm[0:tp, 1, t:t + 1],
                                               ALU.mult, ALU.subtract)
                    last.then_inc(s["fx2n"], 1)
                if e == 5:
                    for k in range(KT):
                        need(dve, s["f2hi"], KT * ch.c + k + 1)
                        low(xTl[:, ch.par, k, 0:R], Fb[k][:, 0:R], xTh[:, ch.par, k, 0:R]).then_inc(s["f2lo"], 1)
                if e == 6 and not end:
                    need(dve, s["frt"], ch.c + 1)
                    a = rl[0:tp, 0:nt, :]
                    sm.step(V.tensor_tensor(a, Fb[0][0:tp, 0:nt * NE].rearrange("p (t e) -> p t e", e=NE),
                                            brbc[0:tp, :].unsqueeze(1).broadcast_to([tp, nt, NE]), ALU.add))
                    sm.step(V.tensor_reduce(rq[0:tp, 0, 0:nt], a, AX.X, ALU.max))
                    V.tensor_tensor(a, a, wide(rq[0:tp, 0, 0:nt], [tp, nt, NE]), ALU.subtract).then_inc(s["flg"], 1)
                if e == 6 and end:
                    need(dve, s["fex"], ch.c + 1)
                    need(dve, s["fw3T"], ch.c)
                    a, w = rl[0:tp, 0:nt, :], wts(ch)[0:tp, 0:nt, :]
                    sm.step(V.tensor_reduce(rq[0:tp, 1, 0:nt], a, AX.X, ALU.add))
                    sm.step(V.reciprocal(rq[0:tp, 0, 0:nt], rq[0:tp, 1, 0:nt]))
                    sm.step(V.tensor_tensor(w, a, wide(rq[0:tp, 0, 0:nt], [tp, nt, NE]), ALU.mult))
                    sm.step(copy(rhr[0:tp, 0:nt, :], w))
                    hr = rhr[0:tp, 0:nt, :].bitcast(fp32)
                    copy(w3[0:tp, 0:nt, 0:NE], hr)
                    V.tensor_tensor(w3[0:tp, 0:nt, NE:2 * NE], w, hr, ALU.subtract)
                    copy(w3[0:tp, 0:nt, 2 * NE:3 * NE], hr).then_inc(s["fw3"], 1)
                if e == 7:
                    for b in range(nb):
                        need(dve, s["fbo"], 2 * ch.c + b + 1)
                        ts = range(2 * b, min(2 * b + 2, nt))
                        t0, t1_ = ts[0], ts[-1] + 1
                        a = acc[0:tp, ch.par, t0:t1_, :]
                        V.tensor_tensor(a, a, Fb[b][0:tp, 0:(t1_ - t0) * D].rearrange("p (t d) -> p t d", d=D), ALU.add)\
                            .then_inc(s["fai"], 1)
                assert sm.n == smalls[e, end]

            smalls = {(0, False): 3, (1, False): 2, (2, False): 0, (3, False): 1, (4, False): 0, (5, False): 0,
                      (6, False): 2, (6, True): 4, (7, True): 0}
            OFF, PER = {}, 0
            for key in smalls:
                OFF[key] = PER
                PER += smalls[key]

            for e in range(NE - 1):
                front(chunk(0), e)
            front(chunk(0), NE - 2, end=True)
            front(chunk(0), NE - 1, end=True)
            hid1(chunk(0), 0)

            def chunk_b(ch):
                nxt = None if ch.last else ch.next()
                for e in range(NE):
                    if e + 1 < NE:
                        hid1(ch, e + 1)
                    elif nxt is not None:
                        hid1(nxt, 0)
                    if e > 0:
                        accumulate(ch, e - 1)
                    elif not (isinstance(ch.c, int) and ch.c == 0):
                        accumulate(ch.prev(), NE - 1)
                    if nxt is not None and e < NE - 1:
                        front(nxt, e)
                    hid2(ch, e)
                    if nxt is not None and e >= NE - 2:
                        front(nxt, e, end=True)
            phase_b_loop(dve, chunk_b)
            accumulate(LAST, NE - 1)


_OUTS = [((N, D), "float32")]


def kernel(**inputs):
    import numpy as _np
    import concourse.bacc as _bacc
    from concourse import mybir as _mybir
    from concourse.bass_utils import run_bass_kernel_spmd as _run

    nc = _bacc.Bacc("TRN2", target_bir_lowering=False, num_devices=1)
    arrays, aps = {}, {}
    for name in inputs:
        a = _np.ascontiguousarray(inputs[name])
        arrays[f"in_{name}"] = a
        aps[name] = nc.dram_tensor(f"in_{name}", a.shape, _mybir.dt.from_np(a.dtype), kind="ExternalInput").ap()
    shape, dtype = _OUTS[0]
    out = nc.dram_tensor("out_0", shape, _mybir.dt.from_np(_np.dtype(dtype)), kind="ExternalOutput").ap()
    build(nc, aps, out)
    r = _run(nc, [arrays], core_ids=[0])
    return r.results[0]["out_0"]
```

```python
import concourse.bass as bass
from concourse import mybir
from contextlib import ExitStack

fp32 = mybir.dt.float32
f32r = mybir.dt.float32r
i32 = mybir.dt.int32
ALU = mybir.AluOpType
ACT = mybir.ActivationFunctionType
AX = mybir.AxisListType

N, D = 6250, 256
P = 128
KT = D // P
CH = 512
TPC = CH // P
NFULL = N // CH
TAIL = N - NFULL * CH
NH, HC = 8, 32
GH, GC = 4, 64
NE = 8
NG = 2 * NH
TAB = D + GH
XTW = D + 2 * GH
WA = 2 * D + XTW
LN_EPS, BN_EPS = 1e-5, 1e-3


class Chunk:

    def __init__(self, c, half, par, rows=CH):
        self.c, self.half, self.par, self.rows = c, half, par, rows
        self.nt = (rows + P - 1) // P
        self.tp = min(rows, P)
        self.last = rows != CH

    @staticmethod
    def at(c):
        return Chunk(c, c // 2, c % 2, CH if c < NFULL else TAIL)

    def next(self):
        if isinstance(self.c, int):
            return Chunk.at(self.c + 1)
        return Chunk(self.c + 1, self.half + self.par, 1 - self.par)

    def prev(self):
        if isinstance(self.c, int):
            return Chunk.at(self.c - 1)
        return Chunk(self.c - 1, self.half - (1 - self.par), 1 - self.par)

    def rows_of(self, dram, nt=None):
        part = dram[bass.ds(self.c * CH, self.rows), :]
        return part.rearrange("(t p) d -> p t d", p=self.tp)


def need(eng, sem, value, alone=None):
    if isinstance(value, int):
        if value > 0:
            eng.wait_ge(sem, value)
        return
    eng.wait_ge(sem, value)
    if alone is not None:
        eng.sem_inc(alone, 1)


class Chain:

    def __init__(self, eng, sem, base=0, alone=None):
        self.eng, self.sem, self.base, self.n, self.alone = eng, sem, base, 0, alone

    def step(self, ins):
        ins.then_inc(self.sem, 1)
        self.n += 1
        need(self.eng, self.sem, self.base + self.n, self.alone)


def build(nc, I, out):
    ctx = ExitStack()
    with ctx:
        def sb(name, shape, dt=fp32):
            return ctx.enter_context(nc.sbuf_tensor(name, shape, dt))

        def sem(name):
            return ctx.enter_context(nc.semaphore(name))

        tab_d = nc.dram_tensor("node_table", (N, TAB), fp32).ap()
        al_d = nc.dram_tensor("node_alpha_l", (N, GH), fp32).ap()

        whi = sb("ffn_w_high", [P, 3 * NE, KT * D], f32r)
        wlo = sb("ffn_w_low", [P, 3 * NE, KT * D], f32r)
        h1h = sb("h1_high", [P, 2, 2, CH], f32r)
        h1l = sb("h1_low", [P, 2, 2, CH], f32r)
        h2 = sb("h2", [P, 2, 2, CH], f32r)
        h2h, h2l = h2[:, 0, :, :], h2[:, 1, :, :]
        tmp = sb("activated", [P, 3, CH])
        xTh = sb("xT_high", [P, 2, KT, CH], f32r)
        xTl = sb("xT_low", [P, 2, KT, CH], f32r)
        xmh = sb("mix_xT_high", [P, KT, CH], f32r)
        xml = sb("mix_xT_low", [P, KT, CH], f32r)
        hmh, hml = xmh, xml
        mwh = sb("mix_w_high", [P, 2, KT, D], f32r)
        mwl = sb("mix_w_low", [P, 2, KT, D], f32r)
        xb = sb("x_rows", [P, 2, TPC, D])
        acc = sb("accumulated", [P, 2, TPC, D])
        xn = sb("normalised", [P, TPC, D])
        base = sb("residual", [P, TPC, D])
        G = sb("gathered", [P, TPC * TAB])
        wst = sb("weight_stage", [P, 3, KT * D])
        wAh = h1h[:, :, :, :].rearrange("p a b c -> p (a b c)")[:, 0:KT * WA].rearrange("p (k n) -> p k n", k=KT)
        wAl = h1l[:, :, :, :].rearrange("p a b c -> p (a b c)")[:, 0:KT * WA].rearrange("p (k n) -> p k n", k=KT)
        kvh, kvl = h2h, h2l
        kvn, sq = tmp[:, 0:2, :], tmp[:, 2, :]
        accf = acc[:, :, :, :].rearrange("p a b c -> p (a b c)")
        wqkv = accf[:, 0:KT * 3 * D].rearrange("p (k n) -> p k n", k=KT)
        w1m = accf[:, KT * 3 * D:KT * 4 * D].rearrange("p (k n) -> p k n", k=KT)
        basef = base[:, :, :].rearrange("p a b -> p (a b)")
        wqT = basef[:, 0:KT * D].rearrange("p (k n) -> p k n", k=KT)
        Pm = basef[:, KT * D:2 * KT * D].rearrange("p (k n) -> p k n", k=KT)
        kvT = xn[:, 2, :].rearrange("p (g n) -> p g n", g=2)
        kvsum = G[:, 0:2 * D]
        xte = G[:, 2 * D:2 * D + 2 * XTW].rearrange("p (a n) -> p a n", a=2)
        gel = xn[:, :, :].rearrange("p (h a) d -> p h (a d)", h=2)
        Gt = G[:, :].rearrange("p (t n) -> p t n", t=TPC)

        ident = sb("identity", [P, P])
        onesf = sb("ones", [P, P])
        onesr = sb("ones_r", [P, P], f32r)
        brow = sb("kv_bias_rows", [P, 2 * D], f32r)
        bo3 = sb("bo_rows", [P, D], f32r)
        wr2 = sb("router_w", [P, KT, 2 * NE], f32r)
        w3T = sb("router_wT", [P, TPC, P], f32r)
        w3 = sb("router_w3", [P, TPC, P])
        b2bc = sb("b2_rows", [P, D])
        brbc = sb("br_rows", [P, NE])
        bnp = sb("bn_cols", [P, 2, 2, 2 * NE])
        c1c = sb("mix_bias_cols", [P, 2])
        b1c = sb("b1_cols", [P, 2])
        bqc = sb("bq_cols", [P, KT])
        gkb = sb("k_gain_rows", [P, HC])
        bkb = sb("k_shift_rows", [P, HC])
        gvc = sb("v_gain_col", [P, 1])
        bvc = sb("v_shift_col", [P, 1])
        mhalf = sb("minus_half", [P, NG])
        rsA = sb("rstd_all", [P, TPC * (NFULL + 1)])
        nmA = sb("shift_all", [P, TPC * (NFULL + 1)])
        st6 = sb("bn_stats", [P, TPC, 6])
        mv = sb("mean_var", [P, TPC, 2])
        rs = sb("rstd", [P, 2, TPC])
        nm = sb("shift", [P, 2, TPC])
        epsc = sb("eps_cols", [P, 2])
        rs1 = sb("rstd_plus_one", [P, TPC])
        ss = sb("sum_squares", [P, 2, NG])
        rk = sb("kv_rstd", [P, 2, NG])
        mn = sb("group_means", [P, NG])
        idx = sb("indices", [P, 2, TPC], i32)
        gal = sb("alpha_l", [P, TPC * GH])
        ga = sb("graph_logits", [P, TPC, GH])
        gs = sb("graph_scalars", [P, 2, TPC])
        rl = sb("router_logits", [P, TPC, NE])
        rq = sb("router_scalars", [P, 2, TPC])
        wpar = [sb(f"router_w{i}", [P, TPC, NE]) for i in range(2)]
        rhr = sb("router_high", [P, TPC, NE], f32r)
        bnr = sb("bn_rows", [4 * NE, 5, P])

        bank = [ctx.enter_context(nc.psum_tensor(f"bank{i}", [P, 512], fp32)) for i in range(8)]
        KVb, XTb, Sb = bank[0:4], bank[4:6], bank[7]
        Tb = bank[6][:, :].rearrange("p (k r) -> p k r", k=KT)
        L1b, L2b, Yb, Fb = bank[0:2], bank[2:4], bank[4:6], bank[6:8]

        names = """ld_w ld_bn ld_small ld_stage id ones eps set_dve set_act set_pool 
            bn_t wq_t wq_ev wst0 wst1 wst2 wst_hi wst_lo
            bn_sq bn_rc x0 x1 stat xsd xrec rstd xnorm tr thi tlo kv xt sq ssum krs krec kvn kvhi kvlo ksum S xte tab0 tab1
            mid_pe mid_dve
            rsl xB0 xB1 fxn fT fThi fTlo fm1 gelu fmh fm2 fx2 fst frs fx2n f2T f2hi f2lo frt flg fex fw3 fw3T fw3c fbo fai
            idx gath glog gexp galpha gbase dsm
            l1 r1 hi1 h1 l2 r2 hi2 h2 y acc out0 out1 passed_pool passed_dve passed_sp""".split()
        s = {n: sem("s_" + n) for n in names}
        s_x = [s["x0"], s["x1"]]
        s_xB = [s["xB0"], s["xB1"]]
        s_wst = [s["wst0"], s["wst1"], s["wst2"]]
        s_tab = [s["tab0"], s["tab1"]]
        s_out = [s["out0"], s["out1"]]

        chunk = Chunk.at
        LAST = chunk(NFULL)
        NTILES = TPC * NFULL + 1

        def mm3(dst, lhs, rhs, lead=False):
            last = None
            n = len(lhs)
            for k in range(n):
                (ah, al), (bh, bl) = lhs[k], rhs[k]
                nc.tensor.matmul(dst, ah, bh, start=(k == 0 and not lead), stop=False)
                nc.tensor.matmul(dst, ah, bl, start=False, stop=False)
                last = nc.tensor.matmul(dst, al, bh, start=False, stop=(k == n - 1))
            return last

        def wide(ap, shape):
            return ap.unsqueeze(len(ap.shape)).broadcast_to(shape)

        def pair(j):
            return Chunk(2 * j + 1, j, 1), Chunk(2 * j + 2, j + 1, 0)

        def phase_a_loop(eng, step, ahead=1):
            step(chunk(0), 0)
            with eng.Fori(0, (NE - 2) // 2) as j:
                for ch in pair(j):
                    step(ch, ch.c)
            if ahead == 1:
                with eng.Fori((NE - 2) // 2, NFULL // 2 - 1) as j:
                    for ch in pair(j):
                        step(ch, None)
            else:
                for c in range(NE - 1, NFULL - 1):
                    step(chunk(c), None)
            step(chunk(NFULL - 1), NE - 1)
            step(LAST, None)

        def phase_b_loop(eng, step, ahead=1):
            step(chunk(0))
            rounds = NFULL // 2 - ahead
            with eng.Fori(0, rounds) as j:
                for ch in pair(j):
                    step(ch)
            for c in range(2 * rounds + 1, NFULL + 1):
                step(chunk(c))

        STAT_TURN = {0: (0, 1), 1: (2, 3)}
        NORM_TURN = {2: (0, 1), 3: (2, 3)}

        def of_next(ch, t, turns):
            if ch.last:
                return []
            return [u for u in turns.get(t, ()) if u < ch.next().nt]

        def to_turn(ch, t):
            if t == 0 and not ch.last:
                return [(ch, 2, 2)]
            if t == TPC - 1:
                return [(ch.next(), 0, min(2, ch.next().nt))]
            return []

        def pair_cols(ch, u, n):
            return slice(u * P, u * P + (n - 1) * P + ch.tp)

        SETUP_A, SETUP_Q, SETUP_POOL = 42, 2, 12
        LD_SMALL = 27
        MID_KV, MID_P, MID = 25, 26, 32

        block = ctx.enter_context(nc.Block())

        @block.sync
        def _(sp):
            def load_x(ch, sems, seen):
                if seen is not None:
                    need(sp, *seen)
                sp.dma_start(xb[0:ch.tp, ch.par, 0:ch.nt, :], ch.rows_of(I["x"])).then_inc(sems[ch.par], 16)

            load_x(chunk(0), s_x, None)
            sp.dma_start(wqkv, I["L0_mix_w_qkv"].rearrange("(k p) n -> p k n", p=P)).then_inc(s["ld_w"], 16)
            sp.dma_start(wst[:, 0, :].rearrange("p (k n) -> p k n", k=KT),
                         I["L0_gnn_weight"].rearrange("(k p) n -> p k n", p=P)).then_inc(s["ld_w"], 16)
            sp.dma_start(wst[:, 1, 0:D], I["L0_gnn_attn_r"].rearrange("a b -> (a b)").partition_broadcast(P)).then_inc(s["ld_w"], 16)
            sp.dma_start(wst[:, 1, D:2 * D], I["L0_gnn_attn_l"].rearrange("a b -> (a b)").partition_broadcast(P)).then_inc(s["ld_w"], 16)
            sp.dma_start(tmp[0:2, 0:2, :].rearrange("p a b -> p (a b)")[:, 0:3 * D],
                         I["L0_mix_b_qkv"].partition_broadcast(2)).then_inc(s["ld_w"], 16)
            load_x(chunk(1), s_x, None)
            for i, n in enumerate(("b1", "g1", "be1", "m1", "v1")):
                for l in range(2):
                    name = "L0_ffn_" + n.replace("1", str(l + 1))
                    sp.dma_start(bnr[2 * NE * l:2 * NE * (l + 1), i, :], I[name].rearrange("e (h p) -> (e h) p", p=P)).then_inc(s["ld_bn"], 16)
            sp.dma_start(w1m, I["L0_mix_w1"].rearrange("(k p) n -> p k n", p=P)).then_inc(s["ld_small"], 16)
            sp.dma_start(rl[:, 0:KT, :], I["L0_ffn_Wr"].rearrange("(k p) e -> p k e", p=P)).then_inc(s["ld_small"], 16)
            for r in range(3):
                sp.dma_start(tmp[r * NE:(r + 1) * NE, 2, 0:D], I["L0_ffn_bo"]).then_inc(s["ld_small"], 16)
            sp.dma_start(b2bc[:, :], I["L0_mix_b2"].partition_broadcast(P)).then_inc(s["ld_small"], 16)
            sp.dma_start(brbc[:, :], I["L0_ffn_br"].partition_broadcast(P)).then_inc(s["ld_small"], 16)
            sp.dma_start(gkb[:, :], I["L0_mix_kln_g"].partition_broadcast(P)).then_inc(s["ld_small"], 16)
            sp.dma_start(bkb[:, :], I["L0_mix_kln_b"].partition_broadcast(P)).then_inc(s["ld_small"], 16)
            for r in range(P // HC):
                rows = slice(r * HC, (r + 1) * HC)
                sp.dma_start(gvc[rows, :], I["L0_mix_vln_g"].unsqueeze(1)).then_inc(s["ld_small"], 16)
                sp.dma_start(bvc[rows, :], I["L0_mix_vln_b"].unsqueeze(1)).then_inc(s["ld_small"], 16)
                for k in range(KT):
                    head = k * (P // HC) + r
                    sp.dma_start(bqc[rows, k:k + 1],
                                 I["L0_mix_b_qkv"][head * 3 * HC:head * 3 * HC + HC].unsqueeze(1)).then_inc(s["ld_small"], 16)
            for k in range(KT):
                sp.dma_start(b1c[:, k:k + 1], I["L0_mix_b1"][k * P:(k + 1) * P].unsqueeze(1)).then_inc(s["ld_small"], 16)

            need(sp, s["set_dve"], SETUP_A)
            def chunk_a(ch, e):
                if e is not None:
                    for l, name in enumerate(("L0_ffn_W1", "L0_ffn_W2", "L0_ffn_Wo")):
                        need(sp, s["wst_lo"], 3 * (e - 1) + l + 1)
                        src = I[name][bass.ds(e, 1), :, :].rearrange("e (k p) n -> p (e k) n", p=P)
                        sp.dma_start(wst[:, l, :].rearrange("p (k n) -> p k n", k=KT), src).then_inc(s_wst[l], 16)
                if not (isinstance(ch.c, int) and ch.c + 2 > NFULL):
                    if isinstance(ch.c, int):
                        nn = chunk(ch.c + 2)
                    else:
                        nn = Chunk(ch.c + 2, ch.half + 1, ch.par)
                    load_x(nn, s_x, (s["xnorm"], TPC * (ch.c + 1)))
                for t in range(ch.nt):
                    g = TPC * ch.c + t
                    tp = ch.tp
                    need(sp, s["xte"], g + 1)
                    sp.dma_start(tab_d[bass.ds(g * P, tp), :], xte[0:tp, t % 2, 0:TAB]).then_inc(s_tab[t % 2], 16)
                    sp.dma_start(al_d[bass.ds(g * P, tp), :], xte[0:tp, t % 2, TAB:XTW]).then_inc(s_tab[t % 2], 16)
            phase_a_loop(sp, chunk_a, ahead=2)

            need(sp, s["wst_lo"], 3 * NE)
            sp.dma_start(wst[:, 0, :].rearrange("p (k n) -> p k n", k=KT),
                         I["L0_mix_w2"].rearrange("(k p) n -> p k n", p=P)).then_inc(s["ld_stage"], 16)

            def load_idx(ch):
                need(sp, s["gath"], 2 * TPC * 16 * ch.c, alone=s["passed_sp"])
                rows = bass.ds(ch.c * CH, ch.rows)
                for a, name in enumerate(("dst", "src")):
                    sp.dma_start(idx[0:ch.tp, a, 0:ch.nt], I[name][rows].rearrange("(t p) -> p t", p=ch.tp),
                                 allow_slow_non_contiguous=True).then_inc(s["idx"], 16)

            def loads_b(ch):
                need(sp, s["fxn"], ch.c - 1)
                load_x(ch, s_xB, None)
                load_idx(ch)

            def store(ch):
                need(sp, s["acc"], 2 * NE * (ch.c + 1) if not ch.last else 2 * NE * NFULL + NE)
                sp.dma_start(ch.rows_of(out), acc[0:ch.tp, ch.par, 0:ch.nt, :]).then_inc(s_out[ch.par], 16)

            need(sp, s["xnorm"], NTILES)
            loads_b(chunk(0))
            loads_b(chunk(1))

            def chunk_b(ch):
                if not (isinstance(ch.c, int) and ch.c == 0):
                    store(ch.prev())
                if not (isinstance(ch.c, int) and ch.c + 2 > NFULL):
                    loads_b(chunk(ch.c + 2) if isinstance(ch.c, int) else Chunk(ch.c + 2, ch.half + 1, ch.par))
            phase_b_loop(sp, chunk_b, ahead=2)
            store(LAST)
            need(sp, s_out[0], 16 * (NFULL // 2 + 1))
            need(sp, s_out[1], 16 * (NFULL // 2))

        @block.gpsimd
        def _(pool):
            nc.gpsimd.memset(ident[:, :], 0.0).then_inc(s["id"], 1)
            nc.gpsimd.memset(onesf[:, :], 1.0).then_inc(s["ones"], 1)
            nc.gpsimd.memset(epsc[:, 0:1], LN_EPS).then_inc(s["eps"], 1)
            nc.gpsimd.memset(epsc[:, 1:2], BN_EPS).then_inc(s["eps"], 1)
            nc.gpsimd.memset(mhalf[:, :], -0.5).then_inc(s["ones"], 1)
            nc.gpsimd.memset(kvsum, 0.0).then_inc(s["ksum"], 1)
            nc.gpsimd.memset(w3[:, :, :], 0.0).then_inc(s["ones"], 1)
            pool.wait_ge(s["id"], 1)
            nc.gpsimd.affine_select(out=ident[:, :], in_=ident[:, :], compare_op=ALU.not_equal, fill=1.0, base=0,
                                    pattern=[[-1, P]], channel_multiplier=1).then_inc(s["id"], 1)
            pool.wait_ge(s["ones"], 2)
            pch = Chain(pool, s["set_pool"])

            def keep_scalars(ch):
                need(pool, s["rstd"], ch.c + 1, alone=s["passed_pool"])
                cols = bass.ds(TPC * ch.c, ch.nt)
                nc.gpsimd.tensor_copy(rsA[0:ch.tp, cols], rs[0:ch.tp, ch.par, 0:ch.nt]).then_inc(s["rsl"], 1)
                nc.gpsimd.tensor_copy(nmA[0:ch.tp, cols], nm[0:ch.tp, ch.par, 0:ch.nt]).then_inc(s["rsl"], 1)

            pool.wait_ge(s["ld_w"], 16 * 5)
            for k in range(KT):
                pch.step(nc.gpsimd.tensor_copy(Pm[:, k, :].rearrange("p (h d) -> p h d", h=NH),
                                               wqkv[:, k, :].rearrange("p (h c) -> p h c", h=NH)[:, :, 0:HC]))
            assert pch.n == SETUP_Q
            keep_scalars(chunk(0))
            pool.wait_ge(s["ld_bn"], 16 * 10)
            b, g, be, m, v = (bnr[:, i, :] for i in range(5))
            pool.wait_ge(s["bn_rc"], 1)
            pch.step(nc.gpsimd.tensor_tensor(g, g, v, ALU.mult))
            pch.step(nc.gpsimd.tensor_tensor(b, b, m, ALU.subtract))
            pch.step(nc.gpsimd.tensor_tensor(b, b, g, ALU.mult))
            pch.step(nc.gpsimd.tensor_tensor(b, b, be, ALU.add))
            def low(dst, full, high):
                return nc.gpsimd.tensor_tensor(dst, full, high.bitcast(fp32), ALU.subtract)
            pool.wait_ge(s["ld_small"], 16 * LD_SMALL)
            pool.wait_ge(s["set_dve"], 2)
            pch.step(nc.gpsimd.tensor_copy(wr2[:, :, 0:NE], rl[:, 0:KT, :]))
            pch.step(low(wr2[:, :, NE:2 * NE], rl[:, 0:KT, :], wr2[:, :, 0:NE]))
            bo, bo_low = tmp[0:3 * NE, 2, 0:D], tmp[0:3 * NE, 2, D:2 * D]
            pch.step(nc.gpsimd.tensor_copy(bo3[0:3 * NE, :], bo))
            pch.step(low(bo_low, bo, bo3[0:3 * NE, :]))
            pch.step(nc.gpsimd.tensor_copy(bo3[0:3 * NE, :], bo_low))
            pch.step(nc.gpsimd.tensor_copy(bo3[0:2 * NE, :], tmp[0:2 * NE, 2, 0:D]))
            assert pch.n == SETUP_POOL

            def chunk_a(ch, e):
                tp = ch.tp
                for t in range(ch.nt):
                    g = TPC * ch.c + t
                    p = t % 2
                    need(pool, s["kvn"], g + 1, alone=s["passed_pool"])
                    need(pool, s["ksum"], g + 1, alone=s["passed_pool"])
                    nc.gpsimd.tensor_tensor(G[0:tp, 0:2 * D], G[0:tp, 0:2 * D], kvn[0:tp, p, :], ALU.add).then_inc(s["ksum"], 1)
                    if e is not None and t > 0:
                        m = t - 1
                        need(pool, s["wst_hi"], 3 * e + m + 1, alone=s["passed_pool"])
                        nc.gpsimd.tensor_tensor(wlo[:, bass.ds(e + m * NE, 1), :].rearrange("p a n -> p (a n)"), wst[:, m, :],
                                                whi[:, bass.ds(e + m * NE, 1), :].rearrange("p a n -> p (a n)").bitcast(fp32),
                                                ALU.subtract).then_inc(s["wst_lo"], 1)
                    if t == 2:
                        keep_scalars(ch.next())
            phase_a_loop(pool, chunk_a)

            pool.wait_ge(s["tr"], NTILES)
            nc.gpsimd.memset(kvT, 0.0).then_inc(s["ones"], 1)

            pool.wait_ge(s["rsl"], 2 * (NFULL + 1))
            pool.wait_ge(s["xnorm"], NTILES)
            pool.wait_ge(s_tab[0], 32 * (2 * NFULL + 1))
            pool.wait_ge(s_tab[1], 32 * 2 * NFULL)
            pool.wait_ge(s["mid_pe"], 1)

            def gather(ch):
                need(pool, s["idx"], 32 * (ch.c + 1), alone=s["passed_pool"])
                for t in range(ch.nt):
                    nc.gpsimd.indirect_dma_start(G[0:ch.tp, t * TAB:(t + 1) * TAB], None, tab_d,
                                                 bass.IndirectOffsetOnAxis(ap=idx[0:ch.tp, 0, t:t + 1], axis=0)).then_inc(s["gath"], 16)
                    nc.gpsimd.indirect_dma_start(gal[0:ch.tp, t * GH:(t + 1) * GH], None, al_d,
                                                 bass.IndirectOffsetOnAxis(ap=idx[0:ch.tp, 1, t:t + 1], axis=0)).then_inc(s["gath"], 16)

            def scalars(ch):
                tp, nt = ch.tp, ch.nt
                need(pool, s["fxn"], ch.c, alone=s["passed_pool"])
                cols = bass.ds(TPC * ch.c, nt)
                nc.gpsimd.tensor_copy(rs[0:tp, 0, 0:nt], rsA[0:tp, cols]).then_inc(s["rsl"], 1)
                nc.gpsimd.tensor_copy(nm[0:tp, 0, 0:nt], nmA[0:tp, cols]).then_inc(s["rsl"], 1)
                need(pool, s["rsl"], 2 * (NFULL + 1) + 3 * ch.c + 1, alone=s["passed_pool"])
                nc.gpsimd.tensor_scalar(rs1[0:tp, 0:nt], rs[0:tp, 0, 0:nt], 1.0, 1.0, ALU.mult, ALU.add).then_inc(s["rsl"], 1)

            def front(ch, last=False):
                tp, nt = ch.tp, ch.nt
                b = 7 * ch.c
                gb = Chain(pool, s["gbase"], b, alone=s["passed_pool"])
                need(pool, s["fxn"], ch.c + 1, alone=s["passed_pool"])
                gb.step(nc.gpsimd.tensor_tensor(base[0:tp, 0:nt, :], base[0:tp, 0:nt, :],
                                                b2bc[0:tp, :].unsqueeze(1).broadcast_to([tp, nt, D]), ALU.add))
                need(pool, s["galpha"], ch.c + 1, alone=s["passed_pool"])
                heads = Gt[0:tp, 0:nt, 0:D].rearrange("p t (h d) -> p t h d", h=GH)
                gb.step(nc.gpsimd.tensor_tensor(heads, heads, wide(ga[0:tp, 0:nt, :], [tp, nt, GH, GC]), ALU.mult))
                gb.step(nc.gpsimd.tensor_tensor(heads[:, :, 0:2, :], heads[:, :, 0:2, :], heads[:, :, 2:4, :], ALU.add))
                gb.step(nc.gpsimd.tensor_tensor(heads[:, :, 0, :], heads[:, :, 0, :], heads[:, :, 1, :], ALU.add))
                bh = base[0:tp, 0:nt, :].rearrange("p t (h d) -> p t h d", h=GH)
                gb.step(nc.gpsimd.tensor_tensor(bh, bh, heads[:, :, 0, :].unsqueeze(2).broadcast_to([tp, nt, GH, GC]), ALU.add))
                if not last:
                    gather(ch.next())
                    scalars(ch.next())
                need(pool, s["fst"], ch.c + 1, alone=s["passed_pool"])
                gb.step(nc.gpsimd.tensor_scalar(rs[0:tp, 1, 0:nt], mv[0:tp, 0:nt, 1], 1.0, LN_EPS, ALU.mult, ALU.add))
                gb.step(nc.gpsimd.tensor_tensor(rs[0:tp, 1, 0:nt], rs[0:tp, 1, 0:nt], mhalf[0:tp, 0:nt], ALU.pow))
                nc.gpsimd.tensor_tensor(nm[0:tp, 1, 0:nt], mv[0:tp, 0:nt, 0], rs[0:tp, 1, 0:nt], ALU.mult).then_inc(s["frs"], 1)
                assert gb.n == 7

            scalars(chunk(0))
            gather(chunk(0))
            front(chunk(0))
            phase_b_loop(pool, lambda ch: None if ch.last else front(ch.next(), last=ch.next().last), ahead=2)

        @block.scalar
        def _(act):
            def copy(dst, src):
                return nc.scalar.activation(dst, src, ACT.Copy)

            act.wait_ge(s["ones"], 1)
            copy(onesr[:, :], onesf[:, :]).then_inc(s["set_act"], 1)

            act.wait_ge(s["eps"], 2)

            def x_sd(ch):
                need(act, s["stat"], TPC * ch.c + ch.nt)
                if not (isinstance(ch.c, int) and ch.c < 2):
                    need(act, s["xnorm"], TPC * (ch.c - 1))
                    need(act, s["rsl"], 2 * (ch.c - 1))
                nc.scalar.activation(rs[0:ch.tp, ch.par, 0:ch.nt], mv[0:ch.tp, 0:ch.nt, 1], ACT.Sqrt,
                                     bias=epsc[0:ch.tp, 0:1]).then_inc(s["xsd"], 1)

            def xnormed(ch, t):
                g = TPC * ch.c + t
                tp = ch.tp
                need(act, s["rstd"], ch.c + 1)
                need(act, s["tr"], g + 1 - TPC)
                nc.scalar.activation(xn[0:tp, t, :], xb[0:tp, ch.par, t, :], ACT.Identity,
                                     bias=nm[0:tp, ch.par, t:t + 1], scale=rs[0:tp, ch.par, t:t + 1]).then_inc(s["xnorm"], 1)

            def t_hi(ch, u, n):
                need(act, s["tr"], TPC * ch.c + u + n)
                if not (isinstance(ch.c, int) and ch.c < 2):
                    need(act, s["xt"], TPC * (ch.c - 1))
                cols = pair_cols(ch, u, n)
                copy(xTh[:, ch.par, :, cols], Tb[:, :, 0:cols.stop - cols.start]).then_inc(s["thi"], n)

            def kv_sd(g, p, tp):
                need(act, s["ssum"], g + 1)
                need(act, s["kvn"], g - 1)
                nc.scalar.activation(rk[0:tp, p, :], ss[0:tp, p, :], ACT.Sqrt, bias=epsc[0:tp, 0:1],
                                     scale=1.0 / HC).then_inc(s["krs"], 1)

            def kv_hi(g, p, tp):
                need(act, s["kvn"], g + 1)
                need(act, s["S"], g - 1)
                copy(kvh[0:tp, p, :], kvn[0:tp, p, :]).then_inc(s["kvhi"], 1)

            x_sd(chunk(0))
            for t in range(TPC):
                xnormed(chunk(0), t)
            act.wait_ge(s["ld_bn"], 16 * 10)
            nc.scalar.activation(bnr[:, 4, :], bnr[:, 4, :], ACT.Sqrt, bias=epsc[0:4 * NE, 1:2]).then_inc(s["bn_sq"], 1)
            t_hi(chunk(0), 0, 2)
            act.wait_ge(s["wq_t"], 1)
            copy(wqT.rearrange("p a b -> p (a b)"), XTb[1][:, :]).then_inc(s["wq_ev"], 1)
            act.wait_ge(s["bn_t"], 1)
            copy(bnp[:, :, :, :].rearrange("p a l b -> p (a l b)"), XTb[0][:, 0:8 * NE]).then_inc(s["wq_ev"], 1)

            def chunk_a(ch, e):
                tp = ch.tp
                for t in range(ch.nt):
                    g = TPC * ch.c + t
                    p = t % 2
                    if not (isinstance(ch.c, int) and g == 0):
                        kv_sd(g - 1, 1 - p, P)
                    need(act, s["kv"], g + 1)
                    need(act, s["ssum"], g)
                    nc.scalar.activation(sq[0:tp, :], KVb[t][0:tp, :], ACT.Square).then_inc(s["sq"], 1)
                    for of, u, n in to_turn(ch, t):
                        t_hi(of, u, n)
                    need(act, s["xt"], g + 1)
                    need(act, s_tab[p], 32 * (2 * ch.c + t // 2))
                    copy(xte[0:tp, p, :], XTb[p][0:tp, 0:XTW]).then_inc(s["xte"], 1)
                    for u in of_next(ch, t, NORM_TURN):
                        xnormed(ch.next(), u)
                    if not (isinstance(ch.c, int) and g == 0):
                        kv_hi(g - 1, 1 - p, P)
                    if t == 1:
                        x_sd(ch.next())
                    if e is not None and t > 0:
                        m = t - 1
                        need(act, s_wst[m], 16 * (e + 1))
                        copy(whi[:, bass.ds(e + m * NE, 1), :].rearrange("p a n -> p (a n)"), wst[:, m, :]).then_inc(s["wst_hi"], 1)
            phase_a_loop(act, chunk_a)
            kv_sd(NTILES - 1, 0, TAIL)
            kv_hi(NTILES - 1, 0, TAIL)

            act.wait_ge(s["mid_dve"], MID)

            def relu(layer, ch, e, h, guard):
                psum, done = (L1b, s["r1"]) if layer == 0 else (L2b, s["r2"])
                need(act, s["l1"] if layer == 0 else s["l2"], 2 * NE * ch.c + 2 * e + h + 1)
                need(act, *guard)
                col = 2 * e + h
                nc.scalar.activation(tmp[:, h, 0:ch.rows], psum[h][:, 0:ch.rows], ACT.Relu,
                                     bias=bnp[:, 1, layer, col:col + 1],
                                     scale=bnp[:, 0, layer, col:col + 1]).then_inc(done, 1)

            def relu1(ch, e):
                for h in range(2):
                    before = 2 * NE * ch.c + 2 * (e - 2) + h + 1
                    if isinstance(ch.c, int) and ch.c == 0 and e == 1:
                        relu(0, ch, e, h, (s["h1"], h + 1))
                    else:
                        relu(0, ch, e, h, (s["h2"], before))

            def relu2(ch, e):
                for h in range(2):
                    if ch.last and e == NE - 1:
                        relu(1, ch, e, h, (s["h2"], 2 * NE * ch.c + 2 * (e - 1) + h + 1))
                    else:
                        relu(1, ch, e, h, (s["h1"], 2 * NE * ch.c + 2 * (e + 1) + h + 1))

            def front(ch, e):
                tp, nt, R = ch.tp, ch.nt, ch.rows
                if e == 1:
                    need(act, s["glog"], ch.c + 1)
                    nc.scalar.activation(ga[0:tp, 0:nt, :], ga[0:tp, 0:nt, :], ACT.Exp).then_inc(s["gexp"], 1)
                    for k in range(KT):
                        need(act, s["fT"], KT * ch.c + k + 1)
                        need(act, s["fm2"], 2 * ch.c)
                        copy(xmh[:, k, 0:R], Fb[k][:, 0:R]).then_inc(s["fThi"], 1)
                if e == 2:
                    for h in range(2):
                        need(act, s["fm1"], 2 * ch.c + h + 1)
                        need(act, s["fT"], KT * (ch.c + 1))
                        nc.scalar.activation(gel[:, h, 0:R], Fb[h][:, 0:R], ACT.Gelu, bias=c1c[:, h:h + 1]).then_inc(s["gelu"], 1)
                if e == 5:
                    for k in range(KT):
                        need(act, s["f2T"], KT * ch.c + k + 1)
                        need(act, s["l1"], 2 * NE * (ch.c - 1))
                        copy(xTh[:, ch.par, k, 0:R], Fb[k][:, 0:R]).then_inc(s["f2hi"], 1)
                if e == 6:
                    need(act, s["flg"], ch.c + 1)
                    nc.scalar.activation(rl[0:tp, 0:nt, :], rl[0:tp, 0:nt, :], ACT.Exp).then_inc(s["fex"], 1)
                if e == 7:
                    need(act, s["fw3T"], ch.c + 1)
                    need(act, s["fbo"], 2 * ch.c)
                    copy(w3T[:, 0:nt, 0:tp], Fb[1][:, 0:nt * P].rearrange("p (t r) -> p t r", r=P)[:, :, 0:tp]).then_inc(s["fw3c"], 1)

            for e in range(NE - 1):
                front(chunk(0), e)
            relu1(chunk(0), 0)

            def chunk_b(ch):
                nxt = None if ch.last else ch.next()
                for e in range(NE):
                    if e + 1 < NE:
                        relu1(ch, e + 1)
                    elif nxt is not None:
                        relu1(nxt, 0)
                    if e == 0:
                        front(ch, NE - 1)
                    relu2(ch, e)
                    if nxt is not None and e < NE - 1:
                        front(nxt, e)
            phase_b_loop(act, chunk_b)

        @block.tensor
        def _(pe):
            pe.wait_ge(s["id"], 2)

            def transposes(ch, u, n):
                g = TPC * ch.c + u
                need(pe, s["tlo"], g)
                for i in range(n):
                    need(pe, s["xnorm"], g + i + 1)
                    for k in range(KT):
                        last = nc.tensor.transpose(Tb[:, k, i * P:i * P + ch.tp], xn[0:ch.tp, u + i, k * P:(k + 1) * P],
                                                   ident[0:ch.tp, 0:ch.tp])
                last.then_inc(s["tr"], n)

            transposes(chunk(0), 0, 2)
            pe.wait_ge(s["set_pool"], SETUP_Q)
            for k in range(KT):
                for g in range(2):
                    last = nc.tensor.transpose(XTb[1][:, g * D + k * P:g * D + (k + 1) * P],
                                               Pm[:, k, g * P:(g + 1) * P], ident[:, :])
            last.then_inc(s["wq_t"], 1)
            pe.wait_ge(s["set_pool"], SETUP_Q + 4)
            for i, row in enumerate((1, 0)):
                last = nc.tensor.transpose(XTb[0][:, i * 4 * NE:(i + 1) * 4 * NE], bnr[:, row, :], ident[0:4 * NE, 0:4 * NE])
            last.then_inc(s["bn_t"], 1)
            pe.wait_ge(s["set_act"], 1)
            pe.wait_ge(s["set_dve"], SETUP_A)
            pe.wait_ge(s["set_pool"], SETUP_POOL)
            pe.wait_ge(s["wq_ev"], 2)
            pe.wait_ge(s["ksum"], 1)
            nc.tensor.matmul(Sb[:, :], onesf[:, :], kvsum, start=True, stop=False, skip_group_check=True)

            def s_product(g, p, tp, final=False):
                need(pe, s["kvlo"], g + 1)
                for grp in range(2):
                    kc, vc = slice(grp * P, (grp + 1) * P), slice(D + grp * P, D + (grp + 1) * P)
                    dst = Sb[:, grp * 2 * P:(grp + 1) * 2 * P].rearrange("p (a n) -> p a n", a=2)
                    nc.tensor.matmul(dst, kvh[0:tp, p, vc], h2[0:tp, :, p, kc], start=False, stop=False, skip_group_check=True)
                    last = nc.tensor.matmul(dst[:, 0, :], kvl[0:tp, p, vc], kvh[0:tp, p, kc], start=False, stop=final, skip_group_check=True)
                last.then_inc(s["S"], 1)

            def chunk_a(ch, e):
                tp = ch.tp
                for t in range(ch.nt):
                    g = TPC * ch.c + t
                    p = t % 2
                    cols = slice(t * P, t * P + tp)
                    lhs = [(xTh[:, ch.par, k, cols], xTl[:, ch.par, k, cols]) for k in range(KT)]
                    need(pe, s["tlo"], g + 1)
                    need(pe, s["kvn"], g + 1 - TPC)
                    nc.tensor.matmul(KVb[t][0:tp, :], onesr[:, 0:tp], brow[:, :], start=True, stop=False)
                    mm3(KVb[t][0:tp, :], lhs, [(wAh[:, k, 0:2 * D], wAl[:, k, 0:2 * D]) for k in range(KT)],
                        lead=True).then_inc(s["kv"], 1)
                    for of, u, n in to_turn(ch, t):
                        transposes(of, u, n)
                    need(pe, s["xte"], g - 1)
                    mm3(XTb[p][0:tp, 0:XTW], lhs, [(wAh[:, k, 2 * D:WA], wAl[:, k, 2 * D:WA]) for k in range(KT)]).then_inc(s["xt"], 1)
                    if not (isinstance(ch.c, int) and g < 2):
                        s_product(g - 2, p, P)
            phase_a_loop(pe, chunk_a)
            s_product(NTILES - 2, 1, P)
            s_product(NTILES - 1, 0, TAIL, final=True)

            pe.wait_ge(s["ksum"], NTILES + 1)
            pe.wait_ge(s["kvn"], NTILES)
            pe.wait_ge(s["xte"], NTILES)
            nc.tensor.matmul(KVb[0][:, 0:D], onesf[:, :], kvsum[:, 0:D], start=True, stop=True)
            for grp in range(2):
                last = nc.tensor.matmul(KVb[1][:, grp:grp + 1], kvsum[:, D + grp * P:D + (grp + 1) * P], onesf[:, 0:1],
                                        start=True, stop=True)
            last.then_inc(s["mid_pe"], 1)
            pe.wait_ge(s["mid_dve"], MID_KV)
            for grp in range(2):
                last = nc.tensor.matmul(XTb[0][:, grp * D:(grp + 1) * D], kvT[:, grp, :], w1m[:, grp, :], start=True, stop=True)
            last.then_inc(s["mid_pe"], 1)
            pe.wait_ge(s["mid_dve"], MID_P)
            for k in range(KT):
                for grp in range(2):
                    last = nc.tensor.matmul(KVb[0][:, k * D:(k + 1) * D], wqT[:, grp, k * P:(k + 1) * P], Pm[:, grp, :],
                                            start=(grp == 0), stop=(grp == 1))
            last.then_inc(s["mid_pe"], 1)
            for h in range(2):
                for grp in range(2):
                    last = nc.tensor.matmul(KVb[1][:, 8 + h:9 + h], Pm[:, grp, h * P:(h + 1) * P], bqc[:, grp:grp + 1],
                                            start=(grp == 0), stop=(grp == 1))
            last.then_inc(s["mid_pe"], 1)
            pe.wait_ge(s["mid_dve"], MID)

            def W(layer, e, k, lo, hi):
                m = layer * NE + e
                return whi[:, m, k * D + lo:k * D + hi], wlo[:, m, k * D + lo:k * D + hi]

            def L1(ch, e):
                R = ch.rows
                if e == 0:
                    need(pe, s["f2lo"], KT * (ch.c + 1))
                for h in range(2):
                    need(pe, s["r1"], 2 * NE * ch.c + 2 * (e - 1) + h + 1)
                    mm3(L1b[h][:, 0:R], [W(0, e, k, h * P, (h + 1) * P) for k in range(KT)],
                        [(xTh[:, ch.par, k, 0:R], xTl[:, ch.par, k, 0:R]) for k in range(KT)]).then_inc(s["l1"], 1)

            def L2(ch, e):
                R = ch.rows
                for h in range(2):
                    need(pe, s["r2"], 2 * NE * ch.c + 2 * (e - 1) + h + 1)
                    if h == 0:
                        need(pe, s["h1"], 2 * NE * ch.c + 2 * e + 2)
                    mm3(L2b[h][:, 0:R], [W(1, e, k, h * P, (h + 1) * P) for k in range(KT)],
                        [(h1h[:, e % 2, k, 0:R], h1l[:, e % 2, k, 0:R]) for k in range(KT)]).then_inc(s["l2"], 1)

            def L3(ch, e):
                tp = ch.tp
                need(pe, s["h2"], 2 * NE * ch.c + 2 * e + 2)
                nb = (ch.nt + 1) // 2
                for b in range(nb):
                    need(pe, s["acc"], 2 * NE * ch.c + (nb * (e - 1) + b + 1 if ch.last and e > 0 else 2 * (e - 1) + b + 1))
                    for t in range(2 * b, min(2 * b + 2, ch.nt)):
                        cols = slice(t * P, t * P + tp)
                        last = mm3(Yb[b][0:tp, (t % 2) * D:(t % 2 + 1) * D],
                                   [(h2h[:, k, cols], h2l[:, k, cols]) for k in range(KT)], [W(2, e, k, 0, D) for k in range(KT)])
                    last.then_inc(s["y"], 1)

            def turned(ch, src):
                for k in range(KT):
                    for t in range(ch.nt):
                        last = nc.tensor.transpose(Fb[k][:, t * P:t * P + ch.tp], src[0:ch.tp, t, k * P:(k + 1) * P],
                                                   ident[0:ch.tp, 0:ch.tp])
                    yield last

            def front(ch, e, end=False):
                tp, nt, R = ch.tp, ch.nt, ch.rows
                nb = (nt + 1) // 2
                if e == 1:
                    need(pe, s["fxn"], ch.c + 1)
                    need(pe, s["fai"], 2 * ch.c)
                    for last in turned(ch, xn):
                        last.then_inc(s["fT"], 1)
                if e == 2:
                    need(pe, s["fTlo"], KT * (ch.c + 1))
                    for h in range(2):
                        mm3(Fb[h][:, 0:R], [(mwh[:, 0, k, h * P:(h + 1) * P], mwl[:, 0, k, h * P:(h + 1) * P]) for k in range(KT)],
                            [(xmh[:, k, 0:R], xml[:, k, 0:R]) for k in range(KT)]).then_inc(s["fm1"], 1)
                if e == 3:
                    need(pe, s["fmh"], 4 * (ch.c + 1))
                    for b in range(nb):
                        for t in range(2 * b, min(2 * b + 2, nt)):
                            cols = slice(t * P, t * P + tp)
                            last = mm3(Fb[b][0:tp, (t % 2) * D:(t % 2 + 1) * D],
                                       [(hmh[:, k, cols], hml[:, k, cols]) for k in range(KT)],
                                       [(mwh[:, 1, k, :], mwl[:, 1, k, :]) for k in range(KT)])
                        last.then_inc(s["fm2"], 1)
                if e == 5:
                    need(pe, s["fx2n"], ch.c + 1)
                    for last in turned(ch, xn):
                        last.then_inc(s["f2T"], 1)
                if e == 6:
                    need(pe, s["f2lo"], KT * (ch.c + 1))
                    for t in range(nt):
                        cols = slice(t * P, t * P + tp)
                        dst = Fb[0][0:tp, 2 * t * NE:2 * (t + 1) * NE]
                        for k in range(KT):
                            nc.tensor.matmul(dst, xTh[:, ch.par, k, cols], wr2[:, k, :], start=(k == 0), stop=False)
                        for k in range(KT):
                            last = nc.tensor.matmul(dst[:, 0:NE], xTl[:, ch.par, k, cols], wr2[:, k, 0:NE],
                                                    start=False, stop=(k == KT - 1))
                    last.then_inc(s["frt"], 1)
                if e == 7 and not end:
                    need(pe, s["fw3"], ch.c + 1)
                    for t in range(nt):
                        last = nc.tensor.transpose(Fb[1][:, t * P:t * P + tp], w3[0:tp, t, :], ident[0:tp, 0:tp])
                    last.then_inc(s["fw3T"], 1)
                if e == 7 and end:
                    need(pe, s["fw3c"], ch.c + 1)
                    for b in range(nb):
                        for t in range(2 * b, min(2 * b + 2, nt)):
                            last = nc.tensor.matmul(Fb[b][0:tp, (t % 2) * D:(t % 2 + 1) * D], w3T[:, t, 0:tp], bo3[:, :],
                                                    start=True, stop=True)
                        last.then_inc(s["fbo"], 1)

            for e in range(NE - 1):
                front(chunk(0), e)
            L1(chunk(0), 0)
            front(chunk(0), NE - 1)

            def chunk_b(ch):
                nxt = None if ch.last else ch.next()
                for e in range(NE):
                    if e + 1 < NE:
                        L1(ch, e + 1)
                    elif nxt is not None:
                        L1(nxt, 0)
                    if e > 0:
                        L3(ch, e - 1)
                    elif not (isinstance(ch.c, int) and ch.c == 0):
                        L3(ch.prev(), NE - 1)
                    if e == 0:
                        front(ch, NE - 1, end=True)
                    if nxt is not None and e < NE - 1:
                        front(nxt, e)
                    L2(ch, e)
                if nxt is not None:
                    front(nxt, NE - 1)
            phase_b_loop(pe, chunk_b)
            L3(LAST, NE - 1)

        @block.vector
        def _(dve):
            V = nc.vector

            def copy(dst, src):
                return V.tensor_copy(dst, src)

            def low(dst, full, high):
                return V.tensor_tensor(dst, full, high.bitcast(fp32), ALU.subtract)

            def stats(ch, t):
                tp = ch.tp
                V.bn_stats(st6[0:tp, t, :], xb[0:tp, ch.par, t, :]).then_inc(s["dsm"], 1)

            def aggr(ch, t):
                V.bn_aggr(mv[0:ch.tp, t, :], st6[0:ch.tp, t, :]).then_inc(s["stat"], 1)

            def x_rstd(ch):
                tp, nt = ch.tp, ch.nt
                need(dve, s["xsd"], ch.c + 1)
                r, m = rs[0:tp, ch.par, 0:nt], nm[0:tp, ch.par, 0:nt]
                V.reciprocal(r, r).then_inc(s["xrec"], 1)
                need(dve, s["xrec"], ch.c + 1, alone=s["passed_dve"])
                V.scalar_tensor_tensor(m, mv[0:tp, 0:nt, 0], -1.0, r, ALU.mult, ALU.mult).then_inc(s["rstd"], 1)

            def t_lo(ch, u, n):
                need(dve, s["thi"], TPC * ch.c + u + n)
                cols = pair_cols(ch, u, n)
                low(xTl[:, ch.par, :, cols], Tb[:, :, 0:cols.stop - cols.start], xTh[:, ch.par, :, cols]).then_inc(s["tlo"], n)

            def kv_lo(g, p, tp):
                need(dve, s["kvhi"], g + 1)
                low(kvl[0:tp, p, :], kvn[0:tp, p, :], kvh[0:tp, p, :]).then_inc(s["kvlo"], 1)

            def kv_norm(g, p, tp, t):
                need(dve, s["krs"], g + 1)
                V.reciprocal(rk[0:tp, p, :], rk[0:tp, p, :]).then_inc(s["krec"], 1)
                need(dve, s["krec"], g + 1)
                need(dve, s["ksum"], g)
                need(dve, s["kvhi"], g - 1)
                V.tensor_tensor(kvn[0:tp, p, :].rearrange("p (h d) -> p h d", h=NG),
                                KVb[t][0:tp, :].rearrange("p (h d) -> p h d", h=NG),
                                wide(rk[0:tp, p, :], [tp, NG, HC]), ALU.mult).then_inc(s["kvn"], 1)

            def stats_of(ch, tiles):
                need(dve, s_x[ch.par], 16 * (ch.half + 1))
                if not (isinstance(ch.c, int) and ch.c == 0):
                    need(dve, s["xsd"], ch.c)
                for t in tiles:
                    stats(ch, t)
                for t in tiles:
                    need(dve, s["dsm"], TPC * ch.c + tiles[-1] + 1, alone=s["passed_dve"])
                    aggr(ch, t)

            stats_of(chunk(0), range(TPC))
            cc = Chain(dve, s["set_dve"])
            cc.step(V.memset(brow[:, :].bitcast(fp32), 0.0))
            cc.step(V.memset(bo3[:, :].bitcast(fp32), 0.0))
            x_rstd(chunk(0))
            dve.wait_ge(s["ld_w"], 16 * 5)
            wf = wst[:, 2, :]
            def centred(src4, rows, dst_hi, dst_lo):
                for i in range(2):
                    part = src4[:, :, (i + 1) * HC:(i + 2) * HC]
                    m8 = mn[0:rows, i * NH:(i + 1) * NH]
                    cc.step(V.tensor_reduce(m8, part, AX.X, ALU.add))
                    cc.step(V.tensor_scalar(m8, m8, 1.0 / HC, None, ALU.mult))
                    w3d = wf[0:rows, i * D:(i + 1) * D].rearrange("p (h d) -> p h d", h=NH)
                    cc.step(V.tensor_tensor(w3d, part, wide(m8, [rows, NH, HC]), ALU.subtract))
                cc.step(copy(dst_hi, wf[0:rows, 0:2 * D]))
                if dst_lo is not None:
                    cc.step(low(dst_lo, wf[0:rows, 0:2 * D], dst_hi))
            for k in range(KT):
                centred(wqkv[:, k, :].rearrange("p (h c) -> p h c", h=NH), P, wAh[:, k, 0:2 * D], wAl[:, k, 0:2 * D])
            dve.wait_ge(s["bn_sq"], 1)
            V.reciprocal(bnr[:, 4, :], bnr[:, 4, :]).then_inc(s["bn_rc"], 1)
            b4 = tmp[0:2, 0:2, :].rearrange("p a b -> p (a b)")[:, 0:3 * D].rearrange("p (h c) -> p h c", h=NH)
            centred(b4, 2, brow[0:2, :], None)
            cc.step(low(tmp[0:2, 0, :], wf[0:2, 0:2 * D], brow[0:2, :]))
            cc.step(copy(brow[0:2, :], tmp[0:2, 0, :]))
            cc.step(copy(brow[0:1, :], wf[0:1, 0:2 * D]))
            for k in range(KT):
                wk = wst[:, 0, k * D:(k + 1) * D]
                cc.step(copy(wf[:, 0:D], wk))
                for i in range(2):
                    cc.step(V.tensor_tensor(tmp[:, 0, 0:D], wk, wst[:, 1, i * D:(i + 1) * D], ALU.mult))
                    cc.step(V.tensor_reduce(wf[:, D + i * GH:D + (i + 1) * GH],
                                            tmp[:, 0, 0:D].rearrange("p (h d) -> p h d", h=GH), AX.X, ALU.add))
                cc.step(copy(wAh[:, k, 2 * D:WA], wf[:, 0:XTW]))
                cc.step(low(wAl[:, k, 2 * D:WA], wf[:, 0:XTW], wAh[:, k, 2 * D:WA]))
            assert cc.n == SETUP_A
            t_lo(chunk(0), 0, 2)
            def chunk_a(ch, e):
                tp = ch.tp
                for t in range(ch.nt):
                    g = TPC * ch.c + t
                    p = t % 2
                    if not (isinstance(ch.c, int) and g == 0):
                        kv_norm(g - 1, 1 - p, P, (t - 1) % TPC)
                    tiles = of_next(ch, t, STAT_TURN)
                    if tiles:
                        stats_of(ch.next(), tiles)
                    need(dve, s["sq"], g + 1)
                    need(dve, s["krs"], g - 1)
                    V.tensor_reduce(ss[0:tp, p, :], sq[0:tp, :].rearrange("p (h d) -> p h d", h=NG), AX.X, ALU.add).then_inc(s["ssum"], 1)
                    for of, u, n in to_turn(ch, t):
                        t_lo(of, u, n)
                    if not (isinstance(ch.c, int) and g == 0):
                        kv_lo(g - 1, 1 - p, P)
                    if t == 1:
                        x_rstd(ch.next())
            phase_a_loop(dve, chunk_a)
            kv_norm(NTILES - 1, 0, TAIL, 0)
            kv_lo(NTILES - 1, 0, TAIL)

            md = Chain(dve, s["mid_dve"])
            dve.wait_ge(s["S"], NTILES)
            dve.wait_ge(s["mid_pe"], 1)
            dve.wait_ge(s["ones"], 4)
            sv = mn[:, 0:2]
            md.step(copy(sv, KVb[1][:, 0:2]))
            t1, t2 = tmp[:, 0, 0:P], tmp[:, 1, 0:P]
            S2 = tmp[:, 2, 0:2 * P].rearrange("p (g n) -> p g n", g=2)
            Sparts = Sb[:, :].rearrange("p (g a n) -> p g a n", g=2, a=2)
            md.step(copy(S2, Sparts[:, :, 1, :]))
            md.step(V.tensor_tensor(S2, Sparts[:, :, 0, :], S2, ALU.add))
            four = [P, P // HC, HC]
            gk4 = gkb[:, :].unsqueeze(1).broadcast_to(four)
            bk4 = bkb[:, :].unsqueeze(1).broadcast_to(four)
            def v4(ap):
                return ap.rearrange("p (h d) -> p h d", d=HC)
            for grp in range(2):
                md.step(V.tensor_tensor(v4(t1), v4(S2[:, grp, :]), gk4, ALU.mult))
                md.step(V.tensor_scalar(v4(t2), bk4, sv[:, grp:grp + 1], None, ALU.mult))
                md.step(V.tensor_tensor(t1, t1, t2, ALU.add))
                md.step(V.tensor_scalar(t1, t1, gvc[:, :], None, ALU.mult))
                md.step(V.tensor_tensor(v4(t2), v4(KVb[0][:, grp * P:(grp + 1) * P]), gk4, ALU.mult))
                md.step(V.scalar_tensor_tensor(v4(t2), bk4, float(N), v4(t2), ALU.mult, ALU.add))
                md.step(V.scalar_tensor_tensor(t1, t2, bvc[:, :], t1, ALU.mult, ALU.add))
                for h in range(P // HC):
                    b = slice(h * HC, (h + 1) * HC)
                    md.step(V.tensor_scalar(kvT[b, grp, b], tmp[b, 0, b], 1.0 / N, None, ALU.mult))
            assert md.n == MID_KV
            dve.wait_ge(s["mid_pe"], 2)
            md.step(copy(Pm.rearrange("p a b -> p (a b)"), XTb[0][:, :]))
            assert md.n == MID_P
            dve.wait_ge(s["mid_pe"], 3)
            Mf = tmp[:, 0, :]
            md.step(V.tensor_tensor(Mf, KVb[0][:, :], w1m.rearrange("p a b -> p (a b)"), ALU.add))
            mh, ml = (m[:, 0, :, :].rearrange("p a b -> p (a b)") for m in (mwh, mwl))
            md.step(copy(mh, Mf))
            md.step(low(ml, Mf, mh))
            dve.wait_ge(s["ld_stage"], 16)
            mh, ml = (m[:, 1, :, :].rearrange("p a b -> p (a b)") for m in (mwh, mwl))
            md.step(copy(mh, wst[:, 0, :]))
            md.step(low(ml, wst[:, 0, :], mh))
            dve.wait_ge(s["mid_pe"], 4)
            md.step(V.tensor_tensor(c1c[:, :], KVb[1][:, 8:10], b1c[:, :], ALU.add))
            assert md.n == MID

            def hid1(ch, e):
                R = ch.rows
                for h in range(2):
                    n = 2 * NE * ch.c + 2 * e + h
                    need(dve, s["r1"], n + 1)
                    need(dve, s["l2"], 2 * NE * ch.c + 2 * (e - 2) + 2)
                    copy(h1h[:, e % 2, h, 0:R], tmp[:, h, 0:R]).then_inc(s["hi1"], 1)
                    dve.wait_ge(s["hi1"], n + 1)
                    low(h1l[:, e % 2, h, 0:R], tmp[:, h, 0:R], h1h[:, e % 2, h, 0:R]).then_inc(s["h1"], 1)

            def hid2(ch, e):
                R = ch.rows
                for h in range(2):
                    n = 2 * NE * ch.c + 2 * e + h
                    need(dve, s["r2"], n + 1)
                    need(dve, s["y"], 2 * NE * ch.c + (e if ch.last else 2 * e))
                    copy(h2h[:, h, 0:R], tmp[:, h, 0:R]).then_inc(s["hi2"], 1)
                    dve.wait_ge(s["hi2"], n + 1)
                    low(h2l[:, h, 0:R], tmp[:, h, 0:R], h2h[:, h, 0:R]).then_inc(s["h2"], 1)

            def accumulate(ch, e):
                tp, nt = ch.tp, ch.nt
                nb = (nt + 1) // 2
                need(dve, s["fai"], 2 * ch.c + nb)
                for b in range(nb):
                    n = 2 * NE * ch.c + nb * e + b
                    need(dve, s["y"], n + 1)
                    if e > 0:
                        need(dve, s["acc"], n + 1 - nb)
                    for t in range(2 * b, min(2 * b + 2, nt)):
                        a = acc[0:tp, ch.par, t, :]
                        last = V.scalar_tensor_tensor(a, Yb[b][0:tp, (t % 2) * D:(t % 2 + 1) * D], wts(ch)[0:tp, t, e:e + 1], a,
                                                      ALU.mult, ALU.add)
                    last.then_inc(s["acc"], 1)

            def wts(ch):
                return wpar[ch.par]

            def front(ch, e, end=False):
                tp, nt, R = ch.tp, ch.nt, ch.rows
                nb = (nt + 1) // 2
                sm = Chain(dve, s["dsm"], NTILES + PER * ch.c + OFF[e, end])
                if e == 0:
                    need(dve, s_xB[ch.par], 16 * (ch.half + 1))
                    need(dve, s["rsl"], 2 * (NFULL + 1) + 3 * (ch.c + 1))
                    need(dve, s["f2T"], KT * ch.c)
                    need(dve, s["gbase"], 7 * ch.c)
                    for t in range(nt):
                        V.tensor_scalar(xn[0:tp, t, :], xb[0:tp, ch.par, t, :], rs[0:tp, 0, t:t + 1], nm[0:tp, 0, t:t + 1],
                                        ALU.mult, ALU.add)
                        last = V.tensor_scalar(base[0:tp, t, :], xb[0:tp, ch.par, t, :], rs1[0:tp, t:t + 1], nm[0:tp, 0, t:t + 1],
                                               ALU.mult, ALU.add)
                    last.then_inc(s["fxn"], 1)
                    need(dve, s["gath"], 2 * TPC * 16 * ch.c + 2 * nt * 16)
                    a = ga[0:tp, 0:nt, :]
                    sm.step(V.tensor_tensor(a, Gt[0:tp, 0:nt, D:TAB], gal[0:tp, 0:nt * GH].rearrange("p (t h) -> p t h", h=GH), ALU.add))
                    sm.step(V.scalar_tensor_tensor(a, a, 0.01, a, ALU.mult, ALU.max))
                    sm.step(V.tensor_reduce(gs[0:tp, 0, 0:nt], a, AX.X, ALU.max))
                    V.tensor_tensor(a, a, wide(gs[0:tp, 0, 0:nt], [tp, nt, GH]), ALU.subtract).then_inc(s["glog"], 1)
                if e == 1:
                    need(dve, s["gexp"], ch.c + 1)
                    a = ga[0:tp, 0:nt, :]
                    sm.step(V.tensor_reduce(gs[0:tp, 1, 0:nt], a, AX.X, ALU.add))
                    sm.step(V.reciprocal(gs[0:tp, 0, 0:nt], gs[0:tp, 1, 0:nt]))
                    V.tensor_tensor(a, a, wide(gs[0:tp, 0, 0:nt], [tp, nt, GH]), ALU.mult).then_inc(s["galpha"], 1)
                    for k in range(KT):
                        need(dve, s["fThi"], KT * ch.c + k + 1)
                        low(xml[:, k, 0:R], Fb[k][:, 0:R], xmh[:, k, 0:R]).then_inc(s["fTlo"], 1)
                if e == 2:
                    for h in range(2):
                        n = 4 * ch.c + 2 * h
                        need(dve, s["gelu"], 2 * ch.c + h + 1)
                        need(dve, s["fm1"], 2 * ch.c + 2)
                        copy(hmh[:, h, 0:R], gel[:, h, 0:R]).then_inc(s["fmh"], 1)
                        dve.wait_ge(s["fmh"], n + 1)
                        low(hml[:, h, 0:R], gel[:, h, 0:R], hmh[:, h, 0:R]).then_inc(s["fmh"], 1)
                if e == 3:
                    need(dve, s["gbase"], 7 * ch.c + 5)
                    if not (isinstance(ch.c, int) and ch.c < 2):
                        need(dve, s_out[ch.par], 16 * ch.half)
                    for b in range(nb):
                        need(dve, s["fm2"], 2 * ch.c + b + 1)
                        ts = range(2 * b, min(2 * b + 2, nt))
                        t0, t1_ = ts[0], ts[-1] + 1
                        V.tensor_tensor(acc[0:tp, ch.par, t0:t1_, :],
                                        Fb[b][0:tp, 0:(t1_ - t0) * D].rearrange("p (t d) -> p t d", d=D),
                                        base[0:tp, t0:t1_, :], ALU.add).then_inc(s["fx2"], 1)
                    dve.wait_ge(s["fx2"], 2 * ch.c + nb)
                    for t in range(nt):
                        last = V.bn_stats(st6[0:tp, t, :], acc[0:tp, ch.par, t, :])
                    sm.step(last)
                    need(dve, s["frs"], ch.c, alone=s["passed_dve"])
                    for t in range(nt):
                        last = V.bn_aggr(mv[0:tp, t, :], st6[0:tp, t, :])
                    last.then_inc(s["fst"], 1)
                if e == 4:
                    need(dve, s["frs"], ch.c + 1)
                    need(dve, s["fT"], KT * (ch.c + 1))
                    for t in range(nt):
                        last = V.tensor_scalar(xn[0:tp, t, :], acc[0:tp, ch.par, t, :], rs[0:tp, 1, t:t + 1], nm[0:tp, 1, t:t + 1],
                                               ALU.mult, ALU.subtract)
                    last.then_inc(s["fx2n"], 1)
                if e == 5:
                    for k in range(KT):
                        need(dve, s["f2hi"], KT * ch.c + k + 1)
                        low(xTl[:, ch.par, k, 0:R], Fb[k][:, 0:R], xTh[:, ch.par, k, 0:R]).then_inc(s["f2lo"], 1)
                if e == 6 and not end:
                    need(dve, s["frt"], ch.c + 1)
                    a = rl[0:tp, 0:nt, :]
                    parts = Fb[0][0:tp, 0:2 * nt * NE].rearrange("p (t e) -> p t e", e=2 * NE)
                    sm.step(V.tensor_tensor(a, parts[:, :, 0:NE], brbc[0:tp, :].unsqueeze(1).broadcast_to([tp, nt, NE]), ALU.add))
                    sm.step(V.tensor_tensor(a, parts[:, :, NE:2 * NE], a, ALU.add))
                    sm.step(V.tensor_reduce(rq[0:tp, 0, 0:nt], a, AX.X, ALU.max))
                    V.tensor_tensor(a, a, wide(rq[0:tp, 0, 0:nt], [tp, nt, NE]), ALU.subtract).then_inc(s["flg"], 1)
                if e == 6 and end:
                    need(dve, s["fex"], ch.c + 1)
                    need(dve, s["fw3T"], ch.c)
                    a, w = rl[0:tp, 0:nt, :], wts(ch)[0:tp, 0:nt, :]
                    sm.step(V.tensor_reduce(rq[0:tp, 1, 0:nt], a, AX.X, ALU.add))
                    sm.step(V.reciprocal(rq[0:tp, 0, 0:nt], rq[0:tp, 1, 0:nt]))
                    sm.step(V.tensor_tensor(w, a, wide(rq[0:tp, 0, 0:nt], [tp, nt, NE]), ALU.mult))
                    sm.step(copy(rhr[0:tp, 0:nt, :], w))
                    hr = rhr[0:tp, 0:nt, :].bitcast(fp32)
                    copy(w3[0:tp, 0:nt, 0:NE], hr)
                    V.tensor_tensor(w3[0:tp, 0:nt, NE:2 * NE], w, hr, ALU.subtract)
                    copy(w3[0:tp, 0:nt, 2 * NE:3 * NE], hr).then_inc(s["fw3"], 1)
                if e == 7:
                    for b in range(nb):
                        need(dve, s["fbo"], 2 * ch.c + b + 1)
                        ts = range(2 * b, min(2 * b + 2, nt))
                        t0, t1_ = ts[0], ts[-1] + 1
                        a = acc[0:tp, ch.par, t0:t1_, :]
                        V.tensor_tensor(a, a, Fb[b][0:tp, 0:(t1_ - t0) * D].rearrange("p (t d) -> p t d", d=D), ALU.add)\
                            .then_inc(s["fai"], 1)
                assert sm.n == smalls[e, end]

            smalls = {(0, False): 3, (1, False): 2, (2, False): 0, (3, False): 1, (4, False): 0, (5, False): 0,
                      (6, False): 3, (6, True): 4, (7, True): 0}
            OFF, PER = {}, 0
            for key in smalls:
                OFF[key] = PER
                PER += smalls[key]

            for e in range(NE - 1):
                front(chunk(0), e)
            front(chunk(0), NE - 2, end=True)
            hid1(chunk(0), 0)

            def chunk_b(ch):
                nxt = None if ch.last else ch.next()
                for e in range(NE):
                    if e + 1 < NE:
                        hid1(ch, e + 1)
                    elif nxt is not None:
                        hid1(nxt, 0)
                    if e > 0:
                        accumulate(ch, e - 1)
                    elif not (isinstance(ch.c, int) and ch.c == 0):
                        accumulate(ch.prev(), NE - 1)
                    if nxt is not None and e == NE - 1:
                        front(nxt, NE - 2, end=True)
                    if e == 0:
                        front(ch, NE - 1, end=True)
                    hid2(ch, e)
                    if nxt is not None and e < NE - 1:
                        front(nxt, e)
            phase_b_loop(dve, chunk_b)
            accumulate(LAST, NE - 1)


_OUTS = [((N, D), "float32")]


def kernel(**inputs):
    import numpy as _np
    import concourse.bacc as _bacc
    from concourse import mybir as _mybir
    from concourse.bass_utils import run_bass_kernel_spmd as _run

    nc = _bacc.Bacc("TRN2", target_bir_lowering=False, num_devices=1)
    arrays, aps = {}, {}
    for name in inputs:
        a = _np.ascontiguousarray(inputs[name])
        arrays[f"in_{name}"] = a
        aps[name] = nc.dram_tensor(f"in_{name}", a.shape, _mybir.dt.from_np(a.dtype), kind="ExternalInput").ap()
    shape, dtype = _OUTS[0]
    out = nc.dram_tensor("out_0", shape, _mybir.dt.from_np(_np.dtype(dtype)), kind="ExternalOutput").ap()
    build(nc, aps, out)
    r = _run(nc, [arrays], core_ids=[0])
    return r.results[0]["out_0"]
```
